# Optimizing a Trainium2 kernel written in Bass

```python
import numpy as np
import jax
import jax.numpy as jnp

def _softmax(x, axis=-1):
    return jax.nn.softmax(x, axis=axis)

def _gelu(x):
    return jax.nn.gelu(x, approximate=True)

def _silu(x):
    return jax.nn.silu(x)

def _sigmoid(x):
    return jax.nn.sigmoid(x)

def _layernorm(x, axis=-1, eps=1e-05):
    m = jnp.mean(x, axis=axis, keepdims=True)
    v = jnp.var(x, axis=axis, keepdims=True)
    return (x - m) / jnp.sqrt(v + eps)

def _scatter_add(tgt, idx, src, axis=0):
    return tgt.at[idx].add(src)

def _segment_sum(src, seg, n):
    return jax.ops.segment_sum(src, seg, n)
kernel_name = 'mk_xattn_ffn_d1_seqx_r8_882644'

def setup_inputs(seed: int=0):
    np.random.seed(seed)
    _w = jnp.asarray

    def _rec_inputs():
        import jax
        import jax.numpy as jnp
        _rk = jax.random.key(seed)
        x = -0.0003929 + 0.9999 * jax.random.normal(jax.random.fold_in(_rk, 1), (1, 1024, 128), jnp.float32)
        _lenS = 1024 - jax.random.randint(jax.random.fold_in(_rk, 7), (1,), 0, max(1, 1024 // 4) + 1, jnp.int32)
        _lenS2 = 6404 - jax.random.randint(jax.random.fold_in(_rk, 8), (1,), 0, max(1, 6404 // 4) + 1, jnp.int32)
        _ctx_768P = jax.random.normal(jax.random.fold_in(_rk, 11), (1, 16, 96), jnp.float32)
        _ctx_768c = jax.random.dirichlet(jax.random.fold_in(_rk, 511), 0.3 * jnp.ones((16,), jnp.float32), (1, 6404))
        _ctx_768t = jnp.einsum('bsk,bkd->bsd', _ctx_768c, _ctx_768P)
        _ctx_768t = _ctx_768t * jax.lax.rsqrt(jnp.mean(jnp.square(_ctx_768t)) + 1e-12) * 0.953939
        ctx_768 = -0.000630117 + 0.999904 * (_ctx_768t + 0.3 * jax.random.normal(jax.random.fold_in(_rk, 611), (1, 6404, 96), jnp.float32))
        return (x, ctx_768)
    x, ctx_768 = _rec_inputs()

    def _L0_xattn_setup():
        import jax, jax.numpy as jnp
        import numpy as np
        NUM_HEAD = 16
        LN_EPS = 1e-05

        def _layernorm(x, g, b):
            m = jnp.mean(x, axis=-1, keepdims=True)
            v = jnp.var(x, axis=-1, keepdims=True)
            return (x - m) * jax.lax.rsqrt(v + LN_EPS) * g + b
        B, T, N, D, L = (32, 64, 77, 128, 96)
        ks = jax.random.split(jax.random.key(seed), 6)
        s = 0.02
        return {'x': jax.random.normal(ks[0], (B, T, D), jnp.float32), 'xf': jax.random.normal(ks[1], (B, N, L), jnp.float32), 'q_w': jax.random.normal(ks[2], (D, D), jnp.float32) * s, 'q_b': jnp.zeros((D,), jnp.float32), 'k_w': jax.random.normal(ks[3], (L, D), jnp.float32) * s, 'k_b': jnp.zeros((D,), jnp.float32), 'v_w': jax.random.normal(ks[4], (L, D), jnp.float32) * s, 'v_b': jnp.zeros((D,), jnp.float32), 'ln_g': jnp.ones((D,), jnp.float32), 'ln_b': jnp.zeros((D,), jnp.float32), 'tln_g': jnp.ones((L,), jnp.float32), 'tln_b': jnp.zeros((L,), jnp.float32)}
    _L0_xattn_all = _L0_xattn_setup()
    _L0_xattn_in = {k: v for k, v in _L0_xattn_all.items() if k in ('q_w', 'q_b', 'k_w', 'k_b', 'v_w', 'v_b', 'ln_g', 'ln_b', 'tln_g', 'tln_b')}
    del _L0_xattn_all

    def _L0_ffn_setup():
        import jax, jax.numpy as jnp
        import numpy as np
        B, S, D, F, E, R, K = (1, 64, 128, 512, 8, 16, 2)
        SCALING = 32.0 / 16.0
        EPS = 1e-06

        def _forward(x, norm_w, w1, w3, w2, gate_w, a1, b1, a3, b3, a2, b2):
            Bq, Sq, Dq = x.shape
            nx = x * jax.lax.rsqrt(jnp.mean(x * x, axis=-1, keepdims=True) + EPS) * norm_w
            t = nx.reshape(-1, Dq)
            probs = jax.nn.softmax(t @ gate_w.T, axis=-1)
            topw, topi = jax.lax.top_k(probs, K)
            topw = topw / jnp.sum(topw, axis=-1, keepdims=True)
            weights = jnp.sum(jax.nn.one_hot(topi, E, dtype=t.dtype) * topw[..., None], axis=1)
            base1 = t @ w1.T
            base3 = t @ w3.T
            h1 = base1[None] + SCALING * jnp.einsum('etr,efr->etf', jnp.einsum('td,erd->etr', t, a1), b1)
            h3 = base3[None] + SCALING * jnp.einsum('etr,efr->etf', jnp.einsum('td,erd->etr', t, a3), b3)
            act = jax.nn.silu(h1) * h3
            out_e = jnp.einsum('etf,df->etd', act, w2) + SCALING * jnp.einsum('etr,edr->etd', jnp.einsum('etf,erf->etr', act, a2), b2)
            out = jnp.einsum('te,etd->td', weights, out_e)
            return out.reshape(Bq, Sq, Dq)
        key = jax.random.key(seed)
        ks = jax.random.split(key, 12)
        w = lambda k, shape: jax.random.normal(k, shape, dtype=jnp.float32) * 0.02
        return {'x': jax.random.normal(ks[0], (B, S, D), dtype=jnp.float32), 'norm_w': jnp.ones((D,), jnp.float32), 'w1': w(ks[1], (F, D)), 'w3': w(ks[2], (F, D)), 'w2': w(ks[3], (D, F)), 'gate_w': w(ks[4], (E, D)), 'a1': w(ks[5], (E, R, D)), 'b1': w(ks[6], (E, F, R)), 'a3': w(ks[7], (E, R, D)), 'b3': w(ks[8], (E, F, R)), 'a2': w(ks[9], (E, R, F)), 'b2': w(ks[10], (E, D, R))}
    _L0_ffn_all = _L0_ffn_setup()
    _L0_ffn_in = {k: v for k, v in _L0_ffn_all.items() if k in ('norm_w', 'w1', 'w3', 'w2', 'gate_w', 'a1', 'b1', 'a3', 'b3', 'a2', 'b2')}
    del _L0_ffn_all
    return {'x': x, 'ctx_768': ctx_768, 'L0_xattn_q_w': _L0_xattn_in['q_w'], 'L0_xattn_q_b': _L0_xattn_in['q_b'], 'L0_xattn_k_w': _L0_xattn_in['k_w'], 'L0_xattn_k_b': _L0_xattn_in['k_b'], 'L0_xattn_v_w': _L0_xattn_in['v_w'], 'L0_xattn_v_b': _L0_xattn_in['v_b'], 'L0_xattn_ln_g': _L0_xattn_in['ln_g'], 'L0_xattn_ln_b': _L0_xattn_in['ln_b'], 'L0_xattn_tln_g': _L0_xattn_in['tln_g'], 'L0_xattn_tln_b': _L0_xattn_in['tln_b'], 'L0_ffn_norm_w': _L0_ffn_in['norm_w'], 'L0_ffn_w1': _L0_ffn_in['w1'], 'L0_ffn_w3': _L0_ffn_in['w3'], 'L0_ffn_w2': _L0_ffn_in['w2'], 'L0_ffn_gate_w': _L0_ffn_in['gate_w'], 'L0_ffn_a1': _L0_ffn_in['a1'], 'L0_ffn_b1': _L0_ffn_in['b1'], 'L0_ffn_a3': _L0_ffn_in['a3'], 'L0_ffn_b3': _L0_ffn_in['b3'], 'L0_ffn_a2': _L0_ffn_in['a2'], 'L0_ffn_b2': _L0_ffn_in['b2']}

def reference(x, ctx_768, L0_xattn_q_w, L0_xattn_q_b, L0_xattn_k_w, L0_xattn_k_b, L0_xattn_v_w, L0_xattn_v_b, L0_xattn_ln_g, L0_xattn_ln_b, L0_xattn_tln_g, L0_xattn_tln_b, L0_ffn_norm_w, L0_ffn_w1, L0_ffn_w3, L0_ffn_w2, L0_ffn_gate_w, L0_ffn_a1, L0_ffn_b1, L0_ffn_a3, L0_ffn_b3, L0_ffn_a2, L0_ffn_b2):
    import jax
    import jax.numpy as jnp

    def _L0_xattn_ref(x, xf, q_w, q_b, k_w, k_b, v_w, v_b, ln_g, ln_b, tln_g, tln_b):
        import jax, jax.numpy as jnp
        import numpy as np
        NUM_HEAD = 16
        LN_EPS = 1e-05

        def _layernorm(x, g, b):
            m = jnp.mean(x, axis=-1, keepdims=True)
            v = jnp.var(x, axis=-1, keepdims=True)
            return (x - m) * jax.lax.rsqrt(v + LN_EPS) * g + b
        B, T, D = x.shape
        N = xf.shape[1]
        H = NUM_HEAD
        dh = D // H
        xn = _layernorm(x, ln_g, ln_b)
        xfn = _layernorm(xf, tln_g, tln_b)
        q = (xn @ q_w + q_b).reshape(B, T, H, dh)
        k = (xfn @ k_w + k_b).reshape(B, N, H, dh)
        v = (xfn @ v_w + v_b).reshape(B, N, H, dh)
        att = jnp.einsum('bthd,bnhd->btnh', q, k) / np.float32(np.sqrt(dh))
        w = jax.nn.softmax(att, axis=2)
        y = jnp.einsum('btnh,bnhd->bthd', w, v).reshape(B, T, D)
        return y

    def _L0_ffn_ref(x, norm_w, w1, w3, w2, gate_w, a1, b1, a3, b3, a2, b2):
        import jax, jax.numpy as jnp
        import numpy as np
        B, S, D, F, E, R, K = (1, 64, 128, 512, 8, 16, 2)
        SCALING = 32.0 / 16.0
        EPS = 1e-06

        def _forward(x, norm_w, w1, w3, w2, gate_w, a1, b1, a3, b3, a2, b2):
            Bq, Sq, Dq = x.shape
            nx = x * jax.lax.rsqrt(jnp.mean(x * x, axis=-1, keepdims=True) + EPS) * norm_w
            t = nx.reshape(-1, Dq)
            probs = jax.nn.softmax(t @ gate_w.T, axis=-1)
            topw, topi = jax.lax.top_k(probs, K)
            topw = topw / jnp.sum(topw, axis=-1, keepdims=True)
            weights = jnp.sum(jax.nn.one_hot(topi, E, dtype=t.dtype) * topw[..., None], axis=1)
            base1 = t @ w1.T
            base3 = t @ w3.T
            h1 = base1[None] + SCALING * jnp.einsum('etr,efr->etf', jnp.einsum('td,erd->etr', t, a1), b1)
            h3 = base3[None] + SCALING * jnp.einsum('etr,efr->etf', jnp.einsum('td,erd->etr', t, a3), b3)
            act = jax.nn.silu(h1) * h3
            out_e = jnp.einsum('etf,df->etd', act, w2) + SCALING * jnp.einsum('etr,edr->etd', jnp.einsum('etf,erf->etr', act, a2), b2)
            out = jnp.einsum('te,etd->td', weights, out_e)
            return out.reshape(Bq, Sq, Dq)
        return _forward(x, norm_w, w1, w3, w2, gate_w, a1, b1, a3, b3, a2, b2)
    x = x + _L0_xattn_ref(_layernorm(x, axis=-1), ctx_768, L0_xattn_q_w, L0_xattn_q_b, L0_xattn_k_w, L0_xattn_k_b, L0_xattn_v_w, L0_xattn_v_b, L0_xattn_ln_g, L0_xattn_ln_b, L0_xattn_tln_g, L0_xattn_tln_b)
    x = x + _L0_ffn_ref(_layernorm(x, axis=-1), L0_ffn_norm_w, L0_ffn_w1, L0_ffn_w3, L0_ffn_w2, L0_ffn_gate_w, L0_ffn_a1, L0_ffn_b1, L0_ffn_a3, L0_ffn_b3, L0_ffn_a2, L0_ffn_b2)
    return x

_drawn_inputs = setup_inputs


def setup_inputs(seed=0):
    import zlib

    import numpy as np

    out = dict(_drawn_inputs(seed))
    spreads = {'L0_xattn_q_b': (0.0, 0.8),
     'L0_xattn_k_b': (0.0, 0.8),
     'L0_xattn_v_b': (0.0, 0.1),
     'L0_xattn_ln_g': (1.0, 0.6),
     'L0_xattn_ln_b': (0.0, 0.8),
     'L0_xattn_tln_g': (1.0, 0.6),
     'L0_xattn_tln_b': (0.0, 0.39),
     'L0_ffn_norm_w': (1.0, 0.6)}
    factors = {'L0_xattn_q_w': 8.0,
     'L0_xattn_k_w': 8.0,
     'L0_ffn_w1': 3.978,
     'L0_ffn_w3': 3.64,
     'L0_ffn_w2': 3.641,
     'L0_ffn_gate_w': 8.0,
     'L0_ffn_a1': 8.0,
     'L0_ffn_b1': 8.0,
     'L0_ffn_a3': 8.0,
     'L0_ffn_b3': 8.0,
     'L0_ffn_a2': 8.0,
     'L0_ffn_b2': 8.0}
    for name, (base, spread) in spreads.items():
        noise = np.random.default_rng([zlib.crc32(name.encode()), seed]).standard_normal(out[name].shape)
        drawn = base * np.exp(spread * noise) if base else spread * noise
        out[name] = jnp.asarray(drawn.astype(out[name].dtype))
    for name, factor in factors.items():
        out[name] = (out[name] * factor).astype(out[name].dtype)
    return out
```

```python
import numpy as np

import concourse.bass as bass
from concourse import mybir
from contextlib import ExitStack


def xattn_ffn(nc, x, ctx_in, q_w, q_b, k_w, k_b, v_w, v_b, ln_g, ln_b, tln_g, tln_b,
              norm_w, w1, w3, w2, gate_w, a1, b1, a3, b3, a2, b2, out):
    fp32 = mybir.dt.float32
    bf16 = mybir.dt.bfloat16
    ALU = mybir.AluOpType
    ACT = mybir.ActivationFunctionType
    AX = mybir.AxisListType

    T, D = x.shape[1], x.shape[2]
    NK, L = ctx_in.shape[1], ctx_in.shape[2]
    H = 16
    DH = D // H
    TA = T // 128
    NT = NK // 128
    NM = NT * 128
    NL = NK - NM
    HALF = T // 2
    F = w1.shape[0]
    FC = F // 128
    E, R = a1.shape[0], a1.shape[1]
    LN_EPS, RMS_EPS, LORA = 1e-5, 1e-6, 2.0
    QSCALE = float(1.0 / np.sqrt(np.float32(DH)))

    QROW = 32
    KR = QROW + 9 * DH
    VW = 32
    YW = DH + 1
    CT = 8
    CW = CT * 128
    NC = -(-NT // CT)
    MB = 512
    GT = MB // 128
    NB = -(-NM // MB)
    MAXB = NB * TA
    AHEAD = TA
    PR = 5
    PAIRS = NT // 2

    def chunk(c):
        return c * CW, min(CW, NM - c * CW)

    def group(g):
        return g * MB, min(MB, NM - g * MB)

    q_parts = nc.dram_tensor("q_parts", (H, 9 * DH, T), bf16, kind="Internal").ap()
    k_parts = nc.dram_tensor("k_parts", (H, 3 * DH, NM), bf16, kind="Internal").ap()

    ctx = ExitStack()
    with ctx:
        def sb(name, shape, dt=fp32):
            return ctx.enter_context(nc.sbuf_tensor(name, shape, dt))

        def pb(name, shape, dt=fp32):
            return ctx.enter_context(nc.psum_tensor(name, shape, dt))

        def sem(name):
            return ctx.enter_context(nc.semaphore(name))

        x_sb = sb("x_sb", [128, TA, D])
        k_op = [sb(f"k_op{i}", [128, NM], bf16) for i in range(2)]
        q_exp = [sb(f"q_exp{i}", [128, T], bf16) for i in range(2)]
        q_max = [sb(f"q_max{i}", [128, T], bf16) for i in range(2)]
        v_all = sb("v_all", [128, NT, D])
        v_head = [sb(f"v_head{i}", [128, NT, VW]) for i in range(2)]
        probs = sb("probs", [128, PR, T])
        blockmax = sb("blockmax", [128, TA, NB + 1])
        negmax = sb("negmax", [128, TA])
        mparts = sb("mparts", [128, TA, 2], bf16)
        mparts_all = sb("mparts_all", [128, H, TA, 2], bf16)
        left_scores = sb("left_scores", [128, TA, H * NL])
        left_max = sb("left_max", [128, TA, H])
        v_left = sb("v_left", [H * NL, H, YW])
        ident = sb("ident", [128, 128])
        ident_b = sb("ident_b", [128, 128], bf16)
        half_sel = sb("half_sel", [128, 2, YW])

        space1 = sb("space1", [128, 3 * E * F])
        ctx_sb = space1[:, 0:NT * L].rearrange("p (j l) -> p j l", l=L)
        kn_t = space1[0:L + 1, NT * L:NT * L + NM]
        w1e = space1[:, 0:E * F].rearrange("p (e f) -> p e f", e=E)
        w3e = space1[:, E * F:2 * E * F].rearrange("p (e f) -> p e f", e=E)
        w2e = space1[:, 2 * E * F:3 * E * F].rearrange("p (e f) -> p e f", e=E)
        space2 = sb("space2", [128, H * HALF])
        acc_all = space2[:, :].rearrange("p (h t) -> p h t", h=H)
        k_split = [space2[:, 1536 * i:1536 * (i + 1)].bitcast(bf16).rearrange("p (s n) -> p s n", s=3)
                   for i in range(2)]
        q_split = space2[:, 3072:4608].bitcast(bf16).rearrange("p (s n) -> p s n", s=3)
        split_r = space2[:, 4608:5632].rearrange("p (i n) -> p i n", i=2)
        z_sb = space2[:, 5632:6656].rearrange("p (a d) -> p a d", d=D)
        xn_t = space2[:, 6656:7680]

        q_t = sb("q_t", [128, T])
        ctx_left = sb("ctx_left", [NL, L])
        bn = sb("bn", [128, NT, 6])
        stat = sb("stat", [128, 4, NT])
        bnl = sb("bnl", [NL, 6])
        statl = sb("statl", [NL, 4])
        bnx = sb("bnx", [128, TA, 6])
        mvx = sb("mvx", [128, TA, 2])
        rx = sb("rx", [128, 2, TA])
        knl_t = sb("knl_t", [L + 1, NL])
        knl_rep = sb("knl_rep", [L + 1, H, NL])
        kw_sb = sb("kw_sb", [L + 1, D])
        vw_sb = sb("vw_sb", [L + 1, D])
        qw_sb = sb("qw_sb", [D, D])
        cols = sb("cols", [128, 8])
        kl_t = sb("kl_t", [128, NL])
        kl_bd = sb("kl_bd", [128, H, NL])
        head_mask = sb("head_mask", [128, H])
        left_mask = sb("left_mask", [H * NL, H])
        expert_mask = sb("expert_mask", [128, E])
        QB, LNG, LNB, TLG, TLB, NW = range(6)

        probs_w = probs[:, :, :].rearrange("p r t -> p (r t)")
        w_nat = probs_w[:, 0:3 * F].rearrange("p (i f) -> p i f", i=3)
        b_nat = probs_w[:, 3 * F:5 * F].rearrange("p (i c n) -> p i c n", i=2, c=FC)
        b2_nat = sb("b2_nat", [128, E, R])
        a_nat = sb("a_nat", [128, 2, D])
        a2_nat = sb("a2_nat", [128, F])
        gate_nat = sb("gate_nat", [E, D])
        w_t = sb("w_t", [128, 3, F])
        b_t = sb("b_t", [128, 2, F])
        b2_t = sb("b2_t", [128, D])
        gate_t = sb("gate_t", [D, E])
        masked = sb("masked", [128, 2, 3, D])

        t_t = probs_w[:, 0:T]
        act_t = probs_w[:, T:T + 2 * FC * HALF].rearrange("p (i c t) -> p i c t", i=2, c=FC)
        op0_w, op1_w = k_op[0][:, :].bitcast(fp32), k_op[1][:, :].bitcast(fp32)
        left_p = op0_w[:, 0:TA * H * NL].rearrange("p (a n) -> p a n", a=TA)
        left_pt = op0_w[0:H * NL, 512:512 + T]
        tmp = op0_w[:, 1536:1536 + T].rearrange("p (a d) -> p a d", a=TA)
        zt = op1_w[:, 0:T].rearrange("p (a d) -> p a d", a=TA)
        silu_t = op1_w[:, T:T + 2 * HALF].rearrange("p (i t) -> p i t", i=2)
        gt = op1_w[:, T + 2 * HALF:T + 2 * HALF + 8 * TA * E].rearrange("p (i a e) -> p i a e", i=8, a=TA)
        gs = sb("gs", [128, 8, TA])
        rden = sb("rden", [128, 2, H])
        first = sb("first", [128, E])

        SC = pb("SC", [128, 2, T])
        MX = pb("MX", [128, 3, MB])
        AC = pb("AC", [128, HALF])
        SCB = SC[:, :, :].rearrange("p a (b c) -> p (a b) c", c=MB)

        names = ("const_ready masks_ready pool_step x_in w_in qw_in cols_in ctx_in_s ctxl_in ffn_in "
                 "bn_done sd_done xt_ready xn_ready q_ps q_ready q_hi q_mid q_res q_lo "
                 "cvar_done csd_done cn_ready ct_ps kn_ready k_ps k_hi k_res k_mid k_lo "
                 "v_ps v_ready k_stored q_stored lt_ps lt_ready lk_ps lk_ready lv_ps lv_ready lrep_ready "
                 "ls_ps ls_ready prep_ps prep_ready prep_sum masked_ready "
                 "lz_ready lp_ready lpt_ps lpt_ready y_ps y_ready var1_done sd1_done ms_done sd2_done "
                 "tn_ready tt_ps tt_ready lg_ps lg_sub lg_exp gates_ready h_ps silu_ready act_ready "
                 "down_ps down_used out_ready out_stored").split()
        S = {n: sem(n) for n in names}
        k_loaded = [[sem(f"k_loaded{i}_{c}") for c in range(NC)] for i in range(2)]
        q_loaded = sem("q_loaded")
        qm_loaded = sem("qm_loaded")
        st_done = sem("st_done")
        exp_done = sem("exp_done")
        pv_done = sem("pv_done")
        acc_free = sem("acc_free")
        mb_done = sem("mb_done")
        mx_done = sem("mx_done")
        m_ready = sem("m_ready")
        dve_link = sem("dve_link")
        max_link = sem("max_link")
        mt_done = sem("mt_done")
        mrow_ready = sem("mrow_ready")
        vh_ready = sem("vh_ready")
        lm_ready = sem("lm_ready")
        ms_ready = sem("ms_ready")
        PVC = 3

        block = ctx.enter_context(nc.Block())

        @block.sync
        def _(sp):
            cv = ctx_in[0, 0:NM, :].rearrange("(p j) l -> p j l", p=128)
            sp.dma_start(ctx_sb, cv).then_inc(S["ctx_in_s"], 16)
            sp.dma_start(kw_sb[0:L, :], k_w).then_inc(S["w_in"], 16)
            sp.dma_start(kw_sb[L:L + 1, :], k_b.rearrange("(a n) -> a n", a=1)).then_inc(S["w_in"], 16)
            sp.dma_start(vw_sb[0:L, :], v_w).then_inc(S["w_in"], 16)
            sp.dma_start(vw_sb[L:L + 1, :], v_b.rearrange("(a n) -> a n", a=1)).then_inc(S["w_in"], 16)
            for i, w in enumerate((w1, w3)):
                sp.dma_start(w_nat[:, i, :].rearrange("p (c d) -> p c d", c=FC),
                             w.rearrange("(c p) d -> p c d", p=128)).then_inc(S["ffn_in"], 16)
            sp.dma_start(w_nat[:, 2, :], w2).then_inc(S["ffn_in"], 16)
            for i, b in enumerate((b1, b3)):
                for c in range(FC):
                    sp.dma_start(b_nat[:, i, c, :].rearrange("p (e r) -> p e r", e=E),
                                 b[:, c * 128:(c + 1) * 128, :].rearrange("e p r -> p e r")).then_inc(S["ffn_in"], 16)
            sp.dma_start(b2_nat[:, :, :], b2.rearrange("e d r -> d e r")).then_inc(S["ffn_in"], 16)
            for i, a in enumerate((a1, a3)):
                sp.dma_start(a_nat[:, i, :], a.rearrange("e r d -> (e r) d")).then_inc(S["ffn_in"], 16)
            sp.dma_start(a2_nat[:, :], a2.rearrange("e r f -> (e r) f")).then_inc(S["ffn_in"], 16)
            sp.dma_start(gate_nat[:, :], gate_w).then_inc(S["ffn_in"], 16)

            sp.wait_ge(S["q_hi"], 1)
            sp.wait_ge(S["q_mid"], 1)
            sp.wait_ge(S["q_lo"], 1)
            for i in range(3):
                for j in range(3):
                    r0 = (3 * i + j) * DH
                    sp.dma_start(q_parts[:, r0:r0 + DH, :], q_split[:, i, :]).then_inc(S["q_stored"], 16)
            sp.wait_ge(S["q_stored"], 9 * 16)

            def load_q(dst, h, done):
                sp.dma_start(dst[QROW:KR, :], q_parts[h, :, :] if isinstance(h, int) else
                             q_parts[bass.ds(h, 1), :, :].rearrange("a r t -> (a r) t")).then_inc(done, 16)

            def load_k(par, h, c):
                n0, w = chunk(c)
                src = (k_parts[h, :, n0:n0 + w] if isinstance(h, int) else
                       k_parts[bass.ds(h, 1), :, n0:n0 + w].rearrange("a r n -> (a r) n"))
                for i in range(3):
                    r0 = QROW + 3 * DH * i
                    sp.dma_start(k_op[par][r0:r0 + 3 * DH, n0:n0 + w], src).then_inc(k_loaded[par][c], 16)

            sp.wait_ge(S["const_ready"], 1)
            load_q(q_max[0], 0, qm_loaded)
            load_q(q_exp[0], 0, q_loaded)
            sp.wait_ge(qm_loaded, 16)
            load_q(q_max[1], 1, qm_loaded)
            for c in range(NC):
                last_g = min(2 * c + 2, NB)
                sp.wait_ge(S["k_hi"], last_g)
                sp.wait_ge(S["k_mid"], last_g)
                sp.wait_ge(S["k_lo"], last_g)
                n0, w = chunk(c)
                for j in range(3):
                    sp.dma_start(k_parts[:, j * DH:(j + 1) * DH, n0:n0 + w],
                                 k_split[c % 2][:, j, 0:w]).then_inc(S["k_stored"], 16)
                sp.wait_ge(S["k_stored"], 48 * (c + 1))
                load_k(0, 0, c)
            for c in range(NC):
                load_k(1, 1, c)

            def head_loads(h, par, more):
                sp.wait_ge(st_done, h * NT + 1)
                load_q(q_exp[1 - par], h + 1, q_loaded)
                if more:
                    load_q(q_max[par], h + 2, qm_loaded)
                    for c in range(NC):
                        sp.wait_ge(st_done, h * NT + min(CT * (c + 1), NT))
                        load_k(par, h + 2, c)

            with sp.Fori(0, H // 2 - 1) as i:
                head_loads(i * 2, 0, True)
                head_loads(i * 2 + 1, 1, True)
            head_loads(H - 2, 0, False)

            sp.wait_ge(S["out_ready"], 1)
            sp.dma_start(out[0].rearrange("(p a) d -> p a d", a=TA), x_sb[:, :, :]).then_inc(S["out_stored"], 16)
            sp.wait_ge(S["out_stored"], 16)

        @block.gpsimd
        def _(pool):
            g = nc.gpsimd
            n = 0

            def step(ins):
                nonlocal n
                n += 1
                ins.then_inc(S["pool_step"], 1)
                pool.wait_ge(S["pool_step"], n)

            def block_mask(m, w):
                step(g.memset(m[:, :], 1.0))
                step(g.affine_select(out=m[:, :], in_=m[:, :], compare_op=ALU.is_ge, fill=0.0, base=0,
                                     pattern=[[-w, m.shape[1]]], channel_multiplier=1))
                step(g.affine_select(out=m[:, :], in_=m[:, :], compare_op=ALU.is_ge, fill=0.0, base=w - 1,
                                     pattern=[[w, m.shape[1]]], channel_multiplier=-1))

            step(g.memset(ident[:, :], 0.0))
            step(g.affine_select(out=ident[:, :], in_=ident[:, :], compare_op=ALU.not_equal, fill=1.0,
                                 base=0, pattern=[[-1, 128]], channel_multiplier=1))
            g.memset(kn_t[L:L + 1, :], 1.0)
            step(g.memset(knl_t[L:L + 1, :], 1.0))
            g.tensor_copy(ident_b[:, :], ident[:, :]).then_inc(S["const_ready"], 1)
            for i in range(2):
                g.memset(q_max[i][0:QROW, :], 0.0)
                g.memset(q_exp[i][0:QROW, :], 0.0)
                step(g.memset(k_op[i][0:QROW, :], 1.0))
            block_mask(head_mask, DH)
            for e in range(E):
                g.memset(first[:, e:e + 1], float(E - e))
            block_mask(left_mask, NL)
            block_mask(expert_mask, R)
            pool.sem_inc(S["masks_ready"], 1)
            step(g.memset(half_sel[:, :, :], 0.0))
            for hf in range(2):
                for q in (hf, 2 + hf):
                    step(g.tensor_copy(half_sel[32 * q:32 * q + 32, hf, :],
                                       ident[32 * q:32 * q + 32, 32 * q:32 * q + YW]))

            pool.wait_ge(S["q_mid"], 1)
            g.tensor_tensor(q_split[:, 2, :], split_r[:, :, :].rearrange("p i n -> p (i n)"),
                            q_split[:, 1, :], ALU.subtract).then_inc(S["q_lo"], 1)
            for gi in range(NB):
                n0, w = group(gi)
                c, o = gi // 2, (gi % 2) * MB
                pool.wait_ge(S["k_mid"], gi + 1)
                g.tensor_tensor(k_split[c % 2][:, 2, o:o + w], split_r[:, gi % 2, 0:w],
                                k_split[c % 2][:, 1, o:o + w], ALU.subtract).then_inc(S["k_lo"], 1)
                if gi == 0:
                    pool.wait_ge(S["lt_ready"], 1)
                    step(g.tensor_copy(knl_rep[:, :, :],
                                       knl_t[:, :].unsqueeze(1).to_broadcast([L + 1, H, NL])))
                    pool.sem_inc(S["lrep_ready"], 1)
                if gi == 1:
                    for i in range(2):
                        step(g.memset(v_head[i][:, :, :], 0.0))
                        step(g.memset(v_head[i][:, :, DH:DH + 1], 1.0))

            def v_copy(par, h):
                g.tensor_copy(v_head[par][:, :, 0:DH], v_all[:, :, bass.ds(h * DH, DH)]).then_inc(vh_ready, 1)

            def left_max_copy(h):
                g.tensor_copy(blockmax[:, :, NB:NB + 1], left_max[:, :, bass.ds(h, 1)]).then_inc(lm_ready, 1)

            def mparts_copy(h):
                g.tensor_copy(mparts_all[:, bass.ds(h, 1), :, :].rearrange("p h a s -> p (h a s)"),
                              mparts[:, :, :].rearrange("p a s -> p (a s)")).then_inc(ms_ready, 1)

            pool.wait_ge(S["ls_ready"], 1)
            left_max_copy(0)
            pool.wait_ge(S["v_ready"], NB)
            v_copy(0, 0)

            pool.wait_ge(S["ffn_in"], 16 * 16)
            pool.wait_ge(S["prep_ready"], 6)
            for e in range(E):
                if e >= 2:
                    pool.wait_ge(S["prep_ps"], 6 + 3 * (e - 1))
                for i, src in enumerate((a_nat[:, 0, :], a_nat[:, 1, :], b2_t[:, :])):
                    ins = g.tensor_scalar(masked[:, e % 2, i, :], src, expert_mask[:, e:e + 1], None, ALU.mult)
                ins.then_inc(S["masked_ready"], 1)
                if e >= 1:
                    pool.wait_ge(S["prep_ready"], 6 + 3 * e)
                    for i, w in enumerate((w1e, w3e, w2e)):
                        g.tensor_tensor(w[:, e - 1, :], w[:, e - 1, :], w_t[:, i, :], ALU.add).then_inc(S["prep_sum"], 1)
            pool.wait_ge(S["prep_ready"], 6 + 3 * E)
            for i, w in enumerate((w1e, w3e, w2e)):
                g.tensor_tensor(w[:, E - 1, :], w[:, E - 1, :], w_t[:, i, :], ALU.add).then_inc(S["prep_sum"], 1)

            def after_max(h, more):
                pool.wait_ge(m_ready, h + 1)
                mparts_copy(h)
                if more:
                    left_max_copy(h + 1)

            def head(h, par, more):
                pool.wait_ge(pv_done, h * PAIRS + PVC)
                v_copy(1 - par, h + 1)
                after_max(h + 1, more)

            after_max(0, True)
            with pool.Fori(0, H // 2 - 1) as i:
                head(i * 2, 0, True)
                head(i * 2 + 1, 1, True)
            head(H - 2, 0, False)

        @block.scalar
        def _(act):
            s = nc.scalar
            act.dma_start(x_sb[:, :, :], x[0].rearrange("(p a) d -> p a d", a=TA)).then_inc(S["x_in"], 16)
            act.dma_start(qw_sb[:, :], q_w).then_inc(S["qw_in"], 16)
            for i, (v, w) in enumerate(((q_b, D), (ln_g, D), (ln_b, D), (tln_g, L), (tln_b, L), (norm_w, D))):
                act.dma_start(cols[0:w, i:i + 1], v.rearrange("(p a) -> p a", a=1)).then_inc(S["cols_in"], 16)
            act.dma_start(ctx_left[:, :], ctx_in[0, NM:NK, :]).then_inc(S["ctxl_in"], 16)

            act.wait_ge(S["bn_done"], 1)
            s.activation(rx[:, 0, :], mvx[:, :, 1], ACT.Sqrt).then_inc(S["sd_done"], 1)
            act.wait_ge(S["bn_done"], 2)
            s.activation(rx[:, 1, :], mvx[:, :, 1], ACT.Sqrt).then_inc(S["sd_done"], 1)
            act.wait_ge(S["cvar_done"], 1)
            s.activation(statl[:, 2:3], statl[:, 1:2], ACT.Sqrt)
            s.activation(stat[:, 2, :], stat[:, 1, :], ACT.Sqrt).then_inc(S["csd_done"], 1)

            act.wait_ge(S["xt_ready"], 1)
            act.wait_ge(S["cols_in"], 6 * 16)
            s.activation(xn_t, SC[:, 0, :], ACT.Identity, bias=cols[:, LNB:LNB + 1],
                         scale=cols[:, LNG:LNG + 1]).then_inc(S["xn_ready"], 1)
            act.wait_ge(S["q_ready"], 1)
            s.activation(q_split[:, 0, :], q_t[:, :], ACT.Copy).then_inc(S["q_hi"], 1)
            act.wait_ge(S["q_res"], 1)
            s.activation(q_split[:, 1, :], split_r[:, :, :].rearrange("p i n -> p (i n)"), ACT.Copy).then_inc(S["q_mid"], 1)

            def kn_evac(gi):
                n0, w = group(gi)
                act.wait_ge(S["ct_ps"], gi + 1)
                s.activation(kn_t[0:L, n0:n0 + w], SCB[0:L, gi % 2, 0:w], ACT.Identity,
                             bias=cols[0:L, TLB:TLB + 1], scale=cols[0:L, TLG:TLG + 1]).then_inc(S["kn_ready"], 1)

            def k_first(gi):
                n0, w = group(gi)
                c, o = gi // 2, (gi % 2) * MB
                act.wait_ge(S["k_ps"], gi + 1)
                if c >= 2:
                    act.wait_ge(S["k_stored"], 48 * (c - 1))
                s.activation(k_split[c % 2][:, 0, o:o + w], SCB[:, 2 + gi % 2, 0:w], ACT.Copy).then_inc(S["k_hi"], 1)

            def k_second(gi):
                n0, w = group(gi)
                c, o = gi // 2, (gi % 2) * MB
                act.wait_ge(S["k_res"], gi + 1)
                s.activation(k_split[c % 2][:, 1, o:o + w], split_r[:, gi % 2, 0:w], ACT.Copy).then_inc(S["k_mid"], 1)

            for gi in range(NB + 2):
                if gi < NB:
                    kn_evac(gi)
                if gi == 1:
                    act.wait_ge(S["lt_ps"], 1)
                    s.activation(knl_t[0:L, :], AC[0:L, 0:NL], ACT.Identity, bias=cols[0:L, TLB:TLB + 1],
                                 scale=cols[0:L, TLG:TLG + 1]).then_inc(S["lt_ready"], 1)
                if 1 <= gi <= NB:
                    k_first(gi - 1)
                if gi >= 2:
                    k_second(gi - 2)

            for i in range(6):
                act.wait_ge(S["prep_ps"], i + 1)
                if i < 3:
                    s.activation(w_t[:, i, :], SCB[:, i % 4, :], ACT.Copy).then_inc(S["prep_ready"], 1)
                elif i < 5:
                    s.activation(b_t[:, i - 3, :], SCB[:, i % 4, :], ACT.Copy).then_inc(S["prep_ready"], 1)
                else:
                    s.activation(b2_t[:, :], SCB[:, i % 4, 0:D], ACT.Copy)
                    s.activation(gate_t[:, :], SCB[:, i % 4, D:D + E], ACT.Copy).then_inc(S["prep_ready"], 1)
            for e in range(E):
                for i, w in enumerate((w1e, w3e, w2e)):
                    k = 6 + 3 * e + i
                    act.wait_ge(S["prep_ps"], k + 1)
                    s.activation(w[:, e, :], SCB[:, k % 4, :], ACT.Copy, scale=LORA).then_inc(S["prep_ready"], 1)

            def m_rows(par, h):
                act.wait_ge(mt_done, h + 1)
                s.activation(q_exp[par][0:2, :], MX[0:2, 2, :].bitcast(bf16), ACT.Copy).then_inc(mrow_ready, 1)

            act.sem_inc(exp_done, 2)
            act.sem_inc(acc_free, 1)
            m_rows(0, 0)

            def head(h, par, next_max):
                for j in range(NT):
                    if j == NT - 2 and next_max:
                        m_rows(1 - par, h + 1)
                    act.wait_ge(st_done, h * NT + j + 1)
                    act.wait_ge(pv_done, h * PAIRS + (j - PR) // 2 + 1 + PVC)
                    s.activation(probs[:, j % PR, :], SC[:, j % 2, :], ACT.Exp).then_inc(exp_done, 1)
                act.wait_ge(pv_done, (h + 1) * PAIRS + PVC)
                dst = (acc_all[:, h, :] if isinstance(h, int) else
                       acc_all[:, bass.ds(h, 1), :].rearrange("p h t -> p (h t)"))
                s.activation(dst, AC[:, :], ACT.Copy).then_inc(acc_free, 1)

            with act.Fori(0, H // 2 - 1) as i:
                head(i * 2, 0, True)
                head(i * 2 + 1, 1, True)
            head(H - 2, 0, True)
            head(H - 1, 1, False)

            act.wait_ge(S["lz_ready"], 1)
            s.activation(left_p, left_scores[:, :, :], ACT.Exp).then_inc(S["lp_ready"], 1)
            act.wait_ge(S["lpt_ps"], 1)
            s.activation(left_pt, MX[0:H * NL, 0:2, :].rearrange("p a b -> p (a b)"), ACT.Copy).then_inc(S["lpt_ready"], 1)
            act.wait_ge(S["var1_done"], 1)
            s.activation(rx[:, 0, :], mvx[:, :, 1], ACT.Sqrt).then_inc(S["sd1_done"], 1)
            act.wait_ge(S["ms_done"], 1)
            s.activation(rx[:, 1, :], gs[:, 0, :], ACT.Sqrt).then_inc(S["sd2_done"], 1)
            act.wait_ge(S["tt_ps"], 1)
            s.activation(t_t, SC[:, 0, :], ACT.Copy, scale=cols[:, NW:NW + 1]).then_inc(S["tt_ready"], 1)
            act.wait_ge(S["lg_sub"], 1)
            s.activation(gt[:, 1, :, :], gt[:, 0, :, :], ACT.Exp).then_inc(S["lg_exp"], 1)
            for n in range(2 * E * FC):
                act.wait_ge(S["h_ps"], n + 1)
                if n >= 2:
                    act.wait_ge(S["act_ready"], n - 1)
                s.activation(silu_t[:, n % 2, :], SC[:, n % 2, 0:HALF], ACT.Silu).then_inc(S["silu_ready"], 1)

        @block.vector
        def _(dve):
            v = nc.vector
            n = 0

            def link(ins):
                nonlocal n
                n += 1
                ins.then_inc(dve_link, 1)
                dve.wait_ge(dve_link, n)

            def stats(src, eps):
                for a in range(TA):
                    v.bn_stats(bnx[:, a, :], src[:, a, :])
                link(v.memset(statl[:, 3:4], 0.0))
                for a in range(TA):
                    v.bn_aggr(mvx[:, a, :], bnx[:, a, :])
                link(v.memset(statl[:, 3:4], 0.0))
                v.tensor_scalar(mvx[:, :, 1], mvx[:, :, 1], eps, None, ALU.add).then_inc(S["bn_done"], 1)

            def normalise(dst, src, i):
                link(v.reciprocal(rx[:, i, :], rx[:, i, :]))
                for a in range(TA):
                    ins = v.tensor_scalar(dst[:, a, :], src[:, a, :], mvx[:, a, 0:1], rx[:, i, a:a + 1],
                                          ALU.subtract, ALU.mult)
                link(ins)

            dve.wait_ge(S["x_in"], 16)
            stats(x_sb, LN_EPS)
            dve.wait_ge(S["sd_done"], 1)
            normalise(z_sb, x_sb, 0)
            stats(z_sb, LN_EPS)
            dve.wait_ge(S["sd_done"], 2)
            normalise(z_sb, z_sb, 1)
            dve.sem_inc(S["xn_ready"], 1)

            dve.wait_ge(S["ctx_in_s"], 16)
            dve.wait_ge(S["ctxl_in"], 16)
            for j in range(NT):
                v.bn_stats(bn[:, j, :], ctx_sb[:, j, :])
            link(v.bn_stats(bnl[:, :], ctx_left[:, :]))
            v.bn_aggr(statl[:, 0:2], bnl[:, :])
            link(v.tensor_tensor(stat[:, 0, :], bn[:, :, 1], bn[:, :, 4], ALU.add))
            link(v.tensor_tensor(stat[:, 1, :], bn[:, :, 1], bn[:, :, 4], ALU.subtract))
            link(v.tensor_tensor(stat[:, 1, :], stat[:, 1, :], stat[:, 1, :], ALU.mult))
            link(v.tensor_tensor(stat[:, 3, :], bn[:, :, 2], bn[:, :, 5], ALU.add))
            link(v.tensor_scalar(stat[:, 3, :], stat[:, 3, :], 1.0 / L, LN_EPS, ALU.mult, ALU.add))
            link(v.tensor_scalar(statl[:, 1:2], statl[:, 1:2], LN_EPS, None, ALU.add))
            v.tensor_scalar(stat[:, 0, :], stat[:, 0, :], 0.5, None, ALU.mult)
            v.scalar_tensor_tensor(stat[:, 1, :], stat[:, 1, :], 0.25, stat[:, 3, :],
                                   ALU.mult, ALU.add).then_inc(S["cvar_done"], 1)

            dve.wait_ge(S["q_ps"], 1)
            link(v.tensor_scalar(q_t[:, :], SC[:, 1, :], cols[:, QB:QB + 1], QSCALE, ALU.add, ALU.mult))
            dve.sem_inc(S["q_ready"], 1)
            dve.wait_ge(S["q_hi"], 1)
            v.tensor_tensor(split_r[:, :, :].rearrange("p i n -> p (i n)"), q_t[:, :], q_split[:, 0, :],
                            ALU.subtract).then_inc(S["q_res"], 1)

            dve.wait_ge(S["csd_done"], 1)
            link(v.reciprocal(stat[:, 3, :], stat[:, 2, :]))
            link(v.reciprocal(statl[:, 3:4], statl[:, 2:3]))
            link(v.tensor_scalar(ctx_left[:, :], ctx_left[:, :], statl[:, 0:1], statl[:, 3:4],
                                 ALU.subtract, ALU.mult))

            def ctx_norm(gi):
                for j in range(gi * GT, min(gi * GT + GT, NT)):
                    ins = v.tensor_scalar(ctx_sb[:, j, :], ctx_sb[:, j, :], stat[:, 0, j:j + 1],
                                          stat[:, 3, j:j + 1], ALU.subtract, ALU.mult)
                ins.then_inc(S["cn_ready"], 1)

            def k_residual(gi):
                n0, w = group(gi)
                c, o = gi // 2, (gi % 2) * MB
                dve.wait_ge(S["k_hi"], gi + 1)
                if gi >= 2:
                    dve.wait_ge(S["k_lo"], gi - 1)
                else:
                    dve.wait_ge(S["q_lo"], 1)
                v.tensor_tensor(split_r[:, gi % 2, 0:w], SCB[:, 2 + gi % 2, 0:w],
                                k_split[c % 2][:, 0, o:o + w], ALU.subtract).then_inc(S["k_res"], 1)

            def v_evac(gi):
                n0, w = group(gi)
                dve.wait_ge(S["v_ps"], gi + 1)
                v.tensor_copy(v_all[:, gi * GT:gi * GT + w // 128, :].rearrange("p j d -> p (j d)"),
                              MX[:, gi % 2, 0:w]).then_inc(S["v_ready"], 1)

            ctx_norm(0)
            ctx_norm(1)
            for gi in range(NB):
                if gi + 2 < NB:
                    ctx_norm(gi + 2)
                k_residual(gi)
                v_evac(gi)
                if gi == 1:
                    dve.wait_ge(S["lk_ps"], 1)
                    dve.wait_ge(S["masks_ready"], 1)
                    link(v.tensor_copy(kl_t[:, :], AC[:, 8:8 + NL]))
                    v.tensor_tensor(kl_bd[:, :, :], kl_t[:, :].unsqueeze(1).to_broadcast([128, H, NL]),
                                    head_mask[:, :].unsqueeze(2).to_broadcast([128, H, NL]),
                                    ALU.mult).then_inc(S["lk_ready"], 1)
                    dve.wait_ge(S["lv_ps"], 1)
                    v.tensor_tensor(v_left[:, :, 0:DH], AC[0:H * NL, 128:256].rearrange("p (h d) -> p h d", h=H),
                                    left_mask[:, :].unsqueeze(2).to_broadcast([H * NL, H, DH]), ALU.mult)
                    v.tensor_copy(v_left[:, :, DH:YW], left_mask[:, :].unsqueeze(2)).then_inc(S["lv_ready"], 1)
                    dve.wait_ge(S["ls_ps"], 1)
                    link(v.tensor_copy(left_scores[:, :, :].rearrange("p a n -> p (a n)"), AC[:, :]))
                    v.tensor_reduce(left_max[:, :, :], left_scores[:, :, :].rearrange("p a (h n) -> p a h n", n=NL),
                                    axis=AX.X, op=ALU.max).then_inc(S["ls_ready"], 1)

            def max_block(h, b):
                kb, a = b // TA, b % TA
                w = min(MB, NM - kb * MB)
                dve.wait_ge(mb_done, h * MAXB + b + 1)
                v.tensor_reduce(blockmax[:, a, kb:kb + 1], MX[:, b % 3, 0:w], axis=AX.X,
                                op=ALU.max).then_inc(mx_done, 1)

            def max_final(h):
                dve.wait_ge(mx_done, (h + 1) * MAXB)
                dve.wait_ge(lm_ready, h + 1)
                dve.wait_ge(ms_ready, h + 1)
                v.tensor_reduce(negmax[:, :], blockmax[:, :, :], axis=AX.X, op=ALU.max,
                                negate=True).then_inc(max_link, 1)
                dve.wait_ge(max_link, h * 2 + 1)
                v.tensor_copy(mparts[:, :, 0], negmax[:, :]).then_inc(max_link, 1)
                dve.wait_ge(max_link, h * 2 + 2)
                v.tensor_tensor(mparts[:, :, 1], negmax[:, :], mparts[:, :, 0], ALU.subtract).then_inc(m_ready, 1)

            dve.sem_inc(ms_ready, 1)
            for b in range(MAXB):
                max_block(0, b)
            max_final(0)
            for b in range(AHEAD):
                max_block(1, b)

            def head(h, more):
                for b in range(AHEAD, MAXB):
                    max_block(h + 1, b)
                max_final(h + 1)
                if more:
                    for b in range(AHEAD):
                        max_block(h + 2, b)

            with dve.Fori(0, H // 2 - 1) as i:
                head(i * 2, True)
                head(i * 2 + 1, True)
            head(H - 2, False)

            dve.wait_ge(ms_ready, H + 1)
            lz = left_scores[:, :, :].rearrange("p a (h n) -> p a h n", n=NL)
            for part in range(2):
                m = mparts_all[:, :, :, part].rearrange("p h a -> p a h").unsqueeze(3)
                ins = v.tensor_tensor(lz, lz, m.to_broadcast([128, TA, H, NL]), ALU.add)
                if part == 0:
                    link(ins)
            ins.then_inc(S["lz_ready"], 1)

            for a in range(TA):
                y = SCB[:, a % 4, 0:H * YW].rearrange("p (h w) -> p h w", w=YW)
                dve.wait_ge(S["y_ps"], a + 1)
                link(v.reciprocal(rden[:, a % 2, :], y[:, :, DH]))
                link(v.tensor_tensor(tmp[:, a, :].rearrange("p (h d) -> p h d", d=DH), y[:, :, 0:DH],
                                     rden[:, a % 2, :].unsqueeze(2).to_broadcast([128, H, DH]), ALU.mult))
                link(v.tensor_tensor(x_sb[:, a, :], x_sb[:, a, :], tmp[:, a, :], ALU.add))
                dve.sem_inc(S["y_ready"], 1)

            for a in range(TA):
                v.bn_stats(bnx[:, a, :], x_sb[:, a, :])
            link(v.memset(statl[:, 3:4], 0.0))
            for a in range(TA):
                v.bn_aggr(mvx[:, a, :], bnx[:, a, :])
            link(v.memset(statl[:, 3:4], 0.0))
            v.tensor_scalar(mvx[:, :, 1], mvx[:, :, 1], LN_EPS, None, ALU.add).then_inc(S["var1_done"], 1)
            dve.wait_ge(S["sd1_done"], 1)
            normalise(zt, x_sb, 0)
            link(v.tensor_tensor(tmp[:, :, :], zt, zt, ALU.mult))
            link(v.tensor_reduce(gs[:, 0, :], tmp[:, :, :], axis=AX.X, op=ALU.add))
            v.tensor_scalar(gs[:, 0, :], gs[:, 0, :], 1.0 / D, RMS_EPS, ALU.mult, ALU.add).then_inc(S["ms_done"], 1)
            dve.wait_ge(S["sd2_done"], 1)
            link(v.reciprocal(rx[:, 1, :], rx[:, 1, :]))
            v.tensor_tensor(zt, zt, rx[:, 1, :].unsqueeze(2).to_broadcast([128, TA, D]),
                            ALU.mult).then_inc(S["tn_ready"], 1)

            def over_e(col):
                return col.unsqueeze(2).to_broadcast([128, TA, E])

            def e_max(dst, src):
                link(v.tensor_reduce(dst, src, axis=AX.X, op=ALU.max))

            lg = MX[:, 2, 0:TA * E].rearrange("p (a e) -> p a e", e=E)
            first_b = first[:, :].unsqueeze(1).to_broadcast([128, TA, E])
            dve.wait_ge(S["lg_ps"], 1)
            e_max(gs[:, 1, :], lg)
            v.tensor_tensor(gt[:, 0, :, :], lg, over_e(gs[:, 1, :]), ALU.subtract).then_inc(S["lg_sub"], 1)
            dve.wait_ge(S["lg_exp"], 1)
            link(v.tensor_reduce(gs[:, 2, :], gt[:, 1, :, :], axis=AX.X, op=ALU.add))
            link(v.reciprocal(gs[:, 2, :], gs[:, 2, :]))
            link(v.tensor_tensor(gt[:, 1, :, :], gt[:, 1, :, :], over_e(gs[:, 2, :]), ALU.mult))
            for top in range(2):
                pr, best = gt[:, 1 + top, :, :], gs[:, 3 + top, :]
                choice = gt[:, 3 + top, :, :]
                e_max(best, pr)
                link(v.tensor_tensor(choice, pr, over_e(best), ALU.is_equal))
                link(v.tensor_tensor(choice, choice, first_b, ALU.mult))
                e_max(gs[:, 5, :], choice)
                link(v.tensor_tensor(choice, choice, over_e(gs[:, 5, :]), ALU.is_equal))
                if top == 0:
                    link(v.scalar_tensor_tensor(gt[:, 2, :, :], choice, -2.0, pr, ALU.mult, ALU.add))
            link(v.tensor_tensor(gs[:, 6, :], gs[:, 3, :], gs[:, 4, :], ALU.add))
            link(v.reciprocal(gs[:, 6, :], gs[:, 6, :]))
            for top in range(2):
                link(v.tensor_tensor(gs[:, 3 + top, :], gs[:, 3 + top, :], gs[:, 6, :], ALU.mult))
                link(v.tensor_tensor(gt[:, 3 + top, :, :], gt[:, 3 + top, :, :], over_e(gs[:, 3 + top, :]), ALU.mult))
            link(v.tensor_tensor(gt[:, 5, :, :], gt[:, 3, :, :], gt[:, 4, :, :], ALU.add))

            def combine(u):
                e, hf = u // 2, u % 2
                dve.wait_ge(S["down_ps"], u + 1)
                for q in range(4):
                    a = hf * 4 + q
                    ins = v.scalar_tensor_tensor(x_sb[:, a, :], MX[:, u % 2, q * 128:(q + 1) * 128],
                                                 gt[:, 5, a, e:e + 1], x_sb[:, a, :], ALU.mult, ALU.add)
                link(ins)
                dve.sem_inc(S["down_used"], 1)

            for u in range(2 * E):
                for c in range(FC):
                    n_h = u * FC + c
                    dve.wait_ge(S["silu_ready"], n_h + 1)
                    if c == 0 and u >= 2:
                        dve.wait_ge(S["down_ps"], u - 1)
                    v.tensor_tensor(act_t[:, u % 2, c, :], silu_t[:, n_h % 2, :], SC[:, n_h % 2, HALF:T],
                                    ALU.mult).then_inc(S["act_ready"], 1)
                if u >= 1:
                    combine(u - 1)
            combine(2 * E - 1)
            dve.sem_inc(S["out_ready"], 1)

        @block.tensor
        def _(pe):
            p = nc.tensor
            pe.wait_ge(S["const_ready"], 1)
            pe.wait_ge(S["xn_ready"], 1)
            for a in range(TA):
                ins = p.transpose(SC[:, 0, a * 128:(a + 1) * 128], z_sb[:, a, :], ident[:, :])
            ins.then_inc(S["xt_ready"], 1)
            pe.wait_ge(S["xn_ready"], 2)
            pe.wait_ge(S["qw_in"], 16)
            for hf in range(2):
                ins = p.matmul(SC[:, 1, hf * HALF:(hf + 1) * HALF], qw_sb[:, :],
                               xn_t[:, hf * HALF:(hf + 1) * HALF], start=True, stop=True)
            ins.then_inc(S["q_ps"], 1)

            def ctx_transpose(gi):
                pe.wait_ge(S["cn_ready"], gi + 1)
                if gi >= 2:
                    pe.wait_ge(S["kn_ready"], gi - 1)
                for j in range(gi * GT, min(gi * GT + GT, NT)):
                    o = (j - gi * GT) * 128
                    ins = p.transpose(SCB[0:L, gi % 2, o:o + 128], ctx_sb[:, j, :], ident[:, :])
                ins.then_inc(S["ct_ps"], 1)

            def k_project(gi):
                n0, w = group(gi)
                pe.wait_ge(S["kn_ready"], gi + 1)
                if gi >= 2:
                    pe.wait_ge(S["k_res"], gi - 1)
                p.matmul(SCB[:, 2 + gi % 2, 0:w], kw_sb[:, :], kn_t[:, n0:n0 + w],
                         start=True, stop=True).then_inc(S["k_ps"], 1)

            def v_project(gi):
                n0, w = group(gi)
                if gi >= 2:
                    pe.wait_ge(S["v_ready"], gi - 1)
                for o in range(0, w, 128):
                    ins = p.matmul(MX[:, gi % 2, o:o + 128], kn_t[:, n0 + o:n0 + o + 128], vw_sb[:, :],
                                   start=True, stop=True)
                ins.then_inc(S["v_ps"], 1)

            pe.wait_ge(S["q_ready"], 1)
            pe.wait_ge(S["w_in"], 4 * 16)
            pe.wait_ge(S["csd_done"], 1)
            ctx_transpose(0)
            p.transpose(AC[0:L, 0:NL], ctx_left[:, :], ident[0:NL, 0:NL]).then_inc(S["lt_ps"], 1)
            for gi in range(NB):
                if gi + 1 < NB:
                    ctx_transpose(gi + 1)
                k_project(gi)
                v_project(gi)
                if gi == 1:
                    pe.wait_ge(S["lt_ready"], 1)
                    p.matmul(AC[:, 8:8 + NL], kw_sb[:, :], knl_t[:, :], start=True, stop=True).then_inc(S["lk_ps"], 1)
                    pe.wait_ge(S["lk_ready"], 1)
                    pe.wait_ge(S["lrep_ready"], 1)
                    p.matmul(AC[0:H * NL, 128:256], knl_rep[:, :, :].rearrange("p h n -> p (h n)"), vw_sb[:, :],
                             start=True, stop=True).then_inc(S["lv_ps"], 1)
                    pe.wait_ge(S["lv_ready"], 1)
                    for a in range(TA):
                        ins = p.matmul(AC[:, a * H * NL:(a + 1) * H * NL], q_t[:, a * 128:(a + 1) * 128],
                                       kl_bd[:, :, :].rearrange("p h n -> p (h n)"), start=True, stop=True)
                    ins.then_inc(S["ls_ps"], 1)

            def prep(k):
                bank = SCB[:, k % 4, :]
                if k == 0:
                    pe.wait_ge(S["ffn_in"], 16 * 16)
                if k >= 4:
                    pe.wait_ge(S["prep_ready"], k - 3)
                else:
                    pe.wait_ge(S["kn_ready"], NB)
                    pe.wait_ge(S["k_res"], NB)
                if k < 3:
                    for c in range(FC):
                        ins = p.transpose(bank[:, c * 128:(c + 1) * 128], w_nat[:, k, c * 128:(c + 1) * 128], ident[:, :])
                elif k < 5:
                    for c in range(FC):
                        ins = p.transpose(bank[:, c * 128:(c + 1) * 128], b_nat[:, k - 3, c, :], ident[:, :])
                elif k == 5:
                    p.transpose(bank[:, 0:D], b2_nat[:, :, :].rearrange("p e r -> p (e r)"), ident[:, :])
                    ins = p.transpose(bank[:, D:D + E], gate_nat[:, :], ident[0:E, 0:E])
                else:
                    e, i = (k - 6) // 3, (k - 6) % 3
                    pe.wait_ge(S["masked_ready"], e + 1)
                    if i < 2:
                        ins = p.matmul(bank, masked[:, e % 2, i, :], b_t[:, i, :], start=True, stop=True)
                    else:
                        for c in range(FC):
                            ins = p.matmul(bank[:, c * 128:(c + 1) * 128], a2_nat[:, c * 128:(c + 1) * 128],
                                           masked[:, e % 2, 2, :], start=True, stop=True)
                ins.then_inc(S["prep_ps"], 1)

            def max_block(par, h, b):
                kb, a = b // TA, b % TA
                n0, w = group(kb)
                if a == 0 and kb % 2 == 0:
                    pe.wait_ge(k_loaded[par][kb // 2], (h + 2 - par) * 24)
                if b == 0:
                    pe.wait_ge(qm_loaded, (h + 1) * 16)
                if b == 2:
                    if not (isinstance(h, int) and h == 0):
                        pe.wait_ge(mrow_ready, h)
                elif not (isinstance(h, int) and h == 0 and b < 2):
                    pe.wait_ge(mx_done, h * MAXB + (b - 2 if b > 2 else b - 1))
                p.matmul(MX[:, b % 3, 0:w], q_max[par][0:KR, a * 128:(a + 1) * 128],
                         k_op[par][0:KR, n0:n0 + w], start=True, stop=True).then_inc(mb_done, 1)

            def max_transpose(h):
                pe.wait_ge(m_ready, h + 1)
                for a in range(TA):
                    ins = p.transpose(MX[0:2, 2, :].bitcast(bf16)[:, a * 128:(a + 1) * 128], mparts[:, a, :],
                                      ident_b[:, :])
                ins.then_inc(mt_done, 1)

            pe.wait_ge(S["v_ready"], NB)
            steps = 6 + 3 * E
            done = 0
            for b in range(MAXB):
                max_block(0, 0, b)
                if b % 3 == 2 and done < steps:
                    prep(done)
                    done += 1
            while done < steps:
                prep(done)
                done += 1
            max_transpose(0)
            for b in range(AHEAD):
                max_block(1, 1, b)
            pe.wait_ge(S["prep_ready"], steps)
            pe.wait_ge(S["ls_ready"], 1)
            pe.sem_inc(pv_done, PVC)

            def scores(par, h, j):
                if j == 0:
                    pe.wait_ge(mrow_ready, h + 1)
                    pe.wait_ge(q_loaded, (h + 1) * 16)
                pe.wait_ge(exp_done, h * NT + j + 1)
                for hf in range(2):
                    ins = p.matmul(SC[:, j % 2, hf * HALF:(hf + 1) * HALF], k_op[par][0:KR, j * 128:(j + 1) * 128],
                                   q_exp[par][0:KR, hf * HALF:(hf + 1) * HALF], start=True, stop=True)
                ins.then_inc(st_done, 1)

            def v_products(par, h, k):
                if k == 0:
                    pe.wait_ge(vh_ready, h + 1)
                    pe.wait_ge(acc_free, h + 1)
                pe.wait_ge(exp_done, h * NT + 2 * k + 2 + 2)
                for q in range(4):
                    j, hf = 2 * k + q // 2, q % 2
                    ins = p.matmul(AC[32 * q:32 * q + VW, :], v_head[par][:, j, :],
                                   probs[:, j % PR, hf * HALF:(hf + 1) * HALF],
                                   start=(k == 0), stop=(k == PAIRS - 1))
                ins.then_inc(pv_done, 1)

            def head(par, h, next_max, more):
                stream = []
                if next_max:
                    stream += [lambda b=b: max_block(1 - par, h + 1, b) for b in range(AHEAD, MAXB)]
                    if more:
                        stream += [lambda b=b: max_block(par, h + 2, b) for b in range(2)]
                        stream += [lambda: max_transpose(h + 1)]
                        stream += [lambda b=b: max_block(par, h + 2, b) for b in range(2, AHEAD)]
                    else:
                        stream += [lambda: max_transpose(h + 1)]
                at = 0
                def some(slot):
                    nonlocal at
                    upto = -(-len(stream) * (slot + 1) // (2 * PAIRS))
                    while at < upto:
                        stream[at]()
                        at += 1
                for k in range(PAIRS):
                    scores(par, h, 2 * k)
                    some(2 * k)
                    scores(par, h, 2 * k + 1)
                    if k >= 1:
                        v_products(par, h, k - 1)
                    some(2 * k + 1)
                v_products(par, h, PAIRS - 1)

            with pe.Fori(0, H // 2 - 1) as i:
                head(0, i * 2, True, True)
                head(1, i * 2 + 1, True, True)
            head(0, H - 2, True, False)
            head(1, H - 1, False, False)

            pe.wait_ge(S["lp_ready"], 1)
            for a in range(TA):
                ins = p.transpose(MX[0:H * NL, a // 4, (a % 4) * 128:(a % 4 + 1) * 128], left_p[:, a, :], ident[:, :])
            ins.then_inc(S["lpt_ps"], 1)
            pe.wait_ge(S["lpt_ready"], 1)
            pe.wait_ge(acc_free, H + 1)
            pe.wait_ge(exp_done, H * NT + 2)
            for a in range(TA):
                if a >= 4:
                    pe.wait_ge(S["y_ready"], a - 3)
                p.matmul(SCB[:, a % 4, 0:H * YW], left_pt[:, a * 128:(a + 1) * 128],
                         v_left[:, :, :].rearrange("p h w -> p (h w)"), start=True, stop=False,
                         skip_group_check=True)
                for h in range(H):
                    ins = p.matmul(SCB[:, a % 4, h * YW:(h + 1) * YW], acc_all[:, h, (a % 4) * 128:(a % 4 + 1) * 128],
                                   half_sel[:, a // 4, :], start=False, stop=(h == H - 1), skip_group_check=True)
                ins.then_inc(S["y_ps"], 1)

            pe.wait_ge(S["tn_ready"], 1)
            for a in range(TA):
                ins = p.transpose(SC[:, 0, a * 128:(a + 1) * 128], zt[:, a, :], ident[:, :])
            ins.then_inc(S["tt_ps"], 1)
            pe.wait_ge(S["tt_ready"], 1)
            for a in range(TA):
                ins = p.matmul(MX[:, 2, a * E:(a + 1) * E], t_t[:, a * 128:(a + 1) * 128], gate_t[:, :],
                               start=True, stop=True)
            ins.then_inc(S["lg_ps"], 1)

            def up(u, c):
                e, hf = u // 2, u % 2
                n_h = u * FC + c
                if n_h >= 2:
                    pe.wait_ge(S["act_ready"], n_h - 1)
                for i, w in enumerate((w1e, w3e)):
                    ins = p.matmul(SC[:, n_h % 2, i * HALF:(i + 1) * HALF], w[:, e, c * 128:(c + 1) * 128],
                                   t_t[:, hf * HALF:(hf + 1) * HALF], start=True, stop=True)
                ins.then_inc(S["h_ps"], 1)

            def down(u):
                e = u // 2
                pe.wait_ge(S["act_ready"], (u + 1) * FC)
                if u >= 2:
                    pe.wait_ge(S["down_used"], u - 1)
                for q in range(4):
                    for c in range(FC):
                        ins = p.matmul(MX[:, u % 2, q * 128:(q + 1) * 128], act_t[:, u % 2, c, q * 128:(q + 1) * 128],
                                       w2e[:, e, c * 128:(c + 1) * 128], start=(c == 0), stop=(c == FC - 1))
                ins.then_inc(S["down_ps"], 1)

            pe.wait_ge(S["prep_sum"], 3 * E)
            for u in range(2 * E):
                for c in range(FC):
                    up(u, c)
                    if u >= 1 and c == 0:
                        down(u - 1)
            down(2 * E - 1)


_INS = ['x', 'ctx_768', 'L0_xattn_q_w', 'L0_xattn_q_b', 'L0_xattn_k_w', 'L0_xattn_k_b', 'L0_xattn_v_w',
        'L0_xattn_v_b', 'L0_xattn_ln_g', 'L0_xattn_ln_b', 'L0_xattn_tln_g', 'L0_xattn_tln_b', 'L0_ffn_norm_w',
        'L0_ffn_w1', 'L0_ffn_w3', 'L0_ffn_w2', 'L0_ffn_gate_w', 'L0_ffn_a1', 'L0_ffn_b1', 'L0_ffn_a3',
        'L0_ffn_b3', 'L0_ffn_a2', 'L0_ffn_b2']


def kernel(**inputs):
    import concourse.bacc as _bacc
    from concourse.bass_utils import run_bass_kernel_spmd as _run

    nc = _bacc.Bacc("TRN2", target_bir_lowering=False, num_devices=1)
    arrays, args = {}, []
    for name in _INS:
        a = np.ascontiguousarray(inputs[name])
        arrays[f"in_{name}"] = a
        args.append(nc.dram_tensor(f"in_{name}", a.shape, mybir.dt.from_np(a.dtype), kind="ExternalInput").ap())
    out = nc.dram_tensor("out_0", tuple(inputs["x"].shape), mybir.dt.float32, kind="ExternalOutput").ap()
    xattn_ffn(nc, *args, out)
    r = _run(nc, [arrays], core_ids=[0])
    return r.results[0]["out_0"]
```

```python
import numpy as np

import concourse.bass as bass
from concourse import mybir
from contextlib import ExitStack


def xattn_ffn(nc, x, ctx_in, q_w, q_b, k_w, k_b, v_w, v_b, ln_g, ln_b, tln_g, tln_b,
              norm_w, w1, w3, w2, gate_w, a1, b1, a3, b3, a2, b2, out):
    fp32 = mybir.dt.float32
    bf16 = mybir.dt.bfloat16
    ALU = mybir.AluOpType
    ACT = mybir.ActivationFunctionType
    AX = mybir.AxisListType

    T, D = x.shape[1], x.shape[2]
    NK, L = ctx_in.shape[1], ctx_in.shape[2]
    H = 16
    DH = D // H
    TA = T // 128
    NT = NK // 128
    NM = NT * 128
    NL = NK - NM
    HALF = T // 2
    F = w1.shape[0]
    FC = F // 128
    E, R = a1.shape[0], a1.shape[1]
    LN_EPS, RMS_EPS, LORA = 1e-5, 1e-6, 2.0
    QSCALE = float(1.0 / np.sqrt(np.float32(DH)))

    QROW = 32
    KR = QROW + 9 * DH
    VW = 32
    YW = DH + 1
    CT = 8
    CW = CT * 128
    NC = -(-NT // CT)
    MB = 512
    GT = MB // 128
    NB = -(-NM // MB)
    MAXB = NB * TA
    AHEAD = TA
    PR = 5
    PAIRS = NT // 2
    TERMS = [(i, j) for i in range(3) for j in range(3)][:128 // R]

    DOWN_LAG = FC + 2

    def chunk(c):
        return c * CW, min(CW, NM - c * CW)

    def group(g):
        return g * MB, min(MB, NM - g * MB)

    q_parts = nc.dram_tensor("q_parts", (H, 9 * DH, T), bf16, kind="Internal").ap()
    y_parts = nc.dram_tensor("y_parts", (2, H, YW, T), fp32, kind="Internal").ap()
    la_parts = nc.dram_tensor("la_parts", (2, 3, E * R, T), bf16, kind="Internal").ap()
    lb_parts = nc.dram_tensor("lb_parts", (2, 3, E * R, F), bf16, kind="Internal").ap()
    k_parts = nc.dram_tensor("k_parts", (H, 3 * DH, NM), bf16, kind="Internal").ap()

    ctx = ExitStack()
    with ctx:
        def sb(name, shape, dt=fp32):
            return ctx.enter_context(nc.sbuf_tensor(name, shape, dt))

        def pb(name, shape, dt=fp32):
            return ctx.enter_context(nc.psum_tensor(name, shape, dt))

        def sem(name):
            return ctx.enter_context(nc.semaphore(name))

        x_sb = sb("x_sb", [128, TA, D])
        k_op = [sb(f"k_op{i}", [128, NM], bf16) for i in range(2)]
        q_exp = [sb(f"q_exp{i}", [128, T], bf16) for i in range(2)]
        q_max = [sb(f"q_max{i}", [128, T], bf16) for i in range(2)]
        v_all = sb("v_all", [128, NT, D])
        v_head = [sb(f"v_head{i}", [128, NT, VW]) for i in range(2)]
        probs = sb("probs", [128, PR, T])
        blockmax = sb("blockmax", [128, TA, NB + 1])
        negmax = sb("negmax", [128, TA])
        mparts = sb("mparts", [128, TA, 2], bf16)
        mparts_all = sb("mparts_all", [128, H, TA, 2], bf16)
        left_scores = sb("left_scores", [128, TA, H * NL])
        left_max = sb("left_max", [128, TA, H])
        v_left = sb("v_left", [H * NL, H * YW])
        ident = sb("ident", [128, 128])
        ident_b = sb("ident_b", [128, 128], bf16)
        den_sel = sb("den_sel", [2 * H, H])
        sums = [sb(f"sums{i}", [128, HALF]) for i in range(2)]

        space1 = sb("space1", [128, 3 * E * F])
        ctx_sb = space1[:, 0:NT * L].rearrange("p (j l) -> p j l", l=L)
        kn_t = space1[0:L + 1, NT * L:NT * L + NM]
        q_t = space1[:, NT * L + NM:NT * L + NM + T]
        lb = space1[:, 0:E * F].bitcast(bf16).rearrange("p (m e f) -> p m e f", m=2, e=E)
        b_split = space1[:, E * F:E * F + 3 * F].bitcast(bf16).rearrange("p (j n) -> p j n", j=3)
        b_res = space1[:, E * F + 3 * F:E * F + 5 * F]
        w2e = space1[:, 2 * E * F:3 * E * F].rearrange("p (e f) -> p e f", e=E)
        space2 = sb("space2", [128, 7680])
        y_num = space2[:, 0:2 * T].rearrange("p (i t) -> p i t", i=2)
        y_den = space2[0:2 * H, 2 * T:3 * T]
        la_split = [space2[:, 1536 * i:1536 * (i + 1)].bitcast(bf16).rearrange("p (s n) -> p s n", s=3)
                    for i in range(2)]
        base = [w.rearrange("p (c m t) -> p c m t", c=FC, m=2)
                for w in (space1[:, E * F:2 * E * F], space2[:, 3 * T:3 * T + E * F])]
        k_split = [space2[:, 1536 * i:1536 * (i + 1)].bitcast(bf16).rearrange("p (s n) -> p s n", s=3)
                   for i in range(2)]
        q_split = space2[:, 3072:4608].bitcast(bf16).rearrange("p (s n) -> p s n", s=3)
        split_r = space2[:, 4608:5632].rearrange("p (i n) -> p i n", i=2)
        z_sb = space2[:, 5632:6656].rearrange("p (a d) -> p a d", d=D)
        xn_t = space2[:, 6656:7680]

        ctx_left = sb("ctx_left", [NL, L])
        bn = sb("bn", [128, NT, 6])
        stat = sb("stat", [128, 4, NT])
        bnl = sb("bnl", [NL, 6])
        statl = sb("statl", [NL, 4])
        bnx = sb("bnx", [128, TA, 6])
        mvx = sb("mvx", [128, TA, 2])
        rx = sb("rx", [128, 2, TA])
        knl_t = sb("knl_t", [L + 1, NL])
        knl_rep = sb("knl_rep", [L + 1, H, NL])
        kw_sb = sb("kw_sb", [L + 1, D])
        vw_sb = sb("vw_sb", [L + 1, D])
        qw_sb = sb("qw_sb", [D, D])
        cols = sb("cols", [128, 8])
        kl_t = sb("kl_t", [128, NL])
        kl_bd = sb("kl_bd", [128, H, NL])
        head_mask = sb("head_mask", [128, H])
        left_mask = sb("left_mask", [H * NL, H])
        expert_mask = sb("expert_mask", [128, E])
        QB, LNG, LNB, TLG, TLB, NW = range(6)

        probs_w = probs[:, :, :].rearrange("p r t -> p (r t)")
        w_nat = probs_w[:, 0:3 * F].rearrange("p (i f) -> p i f", i=3)
        b_nat = probs_w[:, 3 * F:5 * F].rearrange("p (i c n) -> p i c n", i=2, c=FC)
        b2_nat = sb("b2_nat", [128, E, R])
        a_nat = sb("a_nat", [128, 2, D])
        a2_nat = sb("a2_nat", [128, F])
        gate_nat = sb("gate_nat", [E, D])
        w_t = sb("w_t", [128, 3, F])
        b_t = sb("b_t", [128, 2, F])
        b2_t = sb("b2_t", [128, D])
        gate_t = sb("gate_t", [D, E])
        a_t = sb("a_t", [D, 2, E * R])
        masked = sb("masked", [128, 2, D])

        t_t = probs_w[:, 0:T]
        act_t = probs_w[:, T:T + 2 * FC * HALF].rearrange("p (i c t) -> p i c t", i=2, c=FC)
        op0_w, op1_w = k_op[0][:, :].bitcast(fp32), k_op[1][:, :].bitcast(fp32)
        left_p = op0_w[:, 0:TA * H * NL].rearrange("p (a n) -> p a n", a=TA)
        left_pt = op0_w[0:H * NL, 512:512 + T]
        tmp = op0_w[:, 1536:1536 + T].rearrange("p (a d) -> p a d", a=TA)
        zt = op1_w[:, 0:T].rearrange("p (a d) -> p a d", a=TA)
        la_res = [op1_w[:, T:2 * T], op1_w[:, 0:T]]
        uv_t = op0_w[:, 0:2 * T].rearrange("p (i m t) -> p i m t", i=2, m=2)
        silu_t = op0_w[:, 2 * T:3 * T].rearrange("p (i t) -> p i t", i=2)
        v_flat = v_all[:, :, :].rearrange("p j d -> p (j d)")
        la = [w.bitcast(bf16).rearrange("p (m t) -> p m t", m=2)
              for w in [v_flat[:, e * T:(e + 1) * T] for e in range(E - 2)] +
              [v_head[i][:, :, :].rearrange("p j w -> p (j w)")[:, 0:T] for i in range(2)]]
        gt = op1_w[:, T + 2 * HALF:T + 2 * HALF + 8 * TA * E].rearrange("p (i a e) -> p i a e", i=8, a=TA)
        gs = sb("gs", [128, 8, TA])
        rden = sb("rden", [128, 2, H])
        first = sb("first", [128, E])

        SC = pb("SC", [128, 2, T])
        MX = pb("MX", [128, 3, MB])
        AC = pb("AC", [128, HALF])
        SCB = SC[:, :, :].rearrange("p a (b c) -> p (a b) c", c=MB)

        names = ("const_ready masks_ready pool_step x_in w_in qw_in cols_in ctx_in_s ctxl_in ffn_in "
                 "bn_done sd_done xt_ready xn_ready q_ps q_ready q_hi q_mid q_res q_lo "
                 "cvar_done csd_done cn_ready ct_ps kn_ready k_ps k_hi k_res k_mid k_lo "
                 "v_ps v_ready k_stored q_stored lt_ps lt_ready lk_ps lk_ready lv_ps lv_ready lrep_ready "
                 "ls_ps ls_ready prep_ps prep_ready prep_sum masked_ready "
                 "lz_ready lp_ready lpt_ps lpt_ready y_ps y_ready var1_done sd1_done ms_done sd2_done "
                 "tn_ready tt_ps tt_ready lg_ps lg_sub lg_exp gates_ready h_ps silu_ready act_ready "
                 "bt_split b_stored b_loaded la_ps la_hi la_mid la_res_done la_ready la_stored base_ps base_ready uv_ready "
                 "down_ps down_used out_ready out_stored").split()
        S = {n: sem(n) for n in names}
        k_loaded = [[sem(f"k_loaded{i}_{c}") for c in range(NC)] for i in range(2)]
        y_stored = [sem(f"y_stored{i}") for i in range(2)]
        y_loaded = sem("y_loaded")
        la_loaded = [sem(f"la_loaded{e}") for e in range(E)]
        q_loaded = sem("q_loaded")
        qm_loaded = sem("qm_loaded")
        st_done = sem("st_done")
        exp_done = sem("exp_done")
        pv_done = sem("pv_done")
        acc_free = sem("acc_free")
        mb_done = sem("mb_done")
        mx_done = sem("mx_done")
        m_ready = sem("m_ready")
        dve_link = sem("dve_link")
        max_link = sem("max_link")
        mt_done = sem("mt_done")
        mrow_ready = sem("mrow_ready")
        vh_ready = sem("vh_ready")
        lm_ready = sem("lm_ready")
        ms_ready = sem("ms_ready")
        PVC = 3

        block = ctx.enter_context(nc.Block())

        @block.sync
        def _(sp):
            cv = ctx_in[0, 0:NM, :].rearrange("(p j) l -> p j l", p=128)
            sp.dma_start(ctx_sb, cv).then_inc(S["ctx_in_s"], 16)
            sp.dma_start(kw_sb[0:L, :], k_w).then_inc(S["w_in"], 16)
            sp.dma_start(kw_sb[L:L + 1, :], k_b.rearrange("(a n) -> a n", a=1)).then_inc(S["w_in"], 16)
            sp.dma_start(vw_sb[0:L, :], v_w).then_inc(S["w_in"], 16)
            sp.dma_start(vw_sb[L:L + 1, :], v_b.rearrange("(a n) -> a n", a=1)).then_inc(S["w_in"], 16)
            for i, w in enumerate((w1, w3)):
                sp.dma_start(w_nat[:, i, :].rearrange("p (c d) -> p c d", c=FC),
                             w.rearrange("(c p) d -> p c d", p=128)).then_inc(S["ffn_in"], 16)
            sp.dma_start(w_nat[:, 2, :], w2).then_inc(S["ffn_in"], 16)
            for i, b in enumerate((b1, b3)):
                for c in range(FC):
                    sp.dma_start(b_nat[:, i, c, :].rearrange("p (e r) -> p e r", e=E),
                                 b[:, c * 128:(c + 1) * 128, :].rearrange("e p r -> p e r")).then_inc(S["ffn_in"], 16)
            sp.dma_start(b2_nat[:, :, :], b2.rearrange("e d r -> d e r")).then_inc(S["ffn_in"], 16)
            for i, a in enumerate((a1, a3)):
                sp.dma_start(a_nat[:, i, :], a.rearrange("e r d -> (e r) d")).then_inc(S["ffn_in"], 16)
            sp.dma_start(a2_nat[:, :], a2.rearrange("e r f -> (e r) f")).then_inc(S["ffn_in"], 16)
            sp.dma_start(gate_nat[:, :], gate_w).then_inc(S["ffn_in"], 16)

            sp.wait_ge(S["q_hi"], 1)
            sp.wait_ge(S["q_mid"], 1)
            sp.wait_ge(S["q_lo"], 1)
            for i in range(3):
                for j in range(3):
                    r0 = (3 * i + j) * DH
                    sp.dma_start(q_parts[:, r0:r0 + DH, :], q_split[:, i, :]).then_inc(S["q_stored"], 16)
            sp.wait_ge(S["q_stored"], 9 * 16)

            def load_q(dst, h, done):
                sp.dma_start(dst[QROW:KR, :], q_parts[h, :, :] if isinstance(h, int) else
                             q_parts[bass.ds(h, 1), :, :].rearrange("a r t -> (a r) t")).then_inc(done, 16)

            def load_k(par, h, c):
                n0, w = chunk(c)
                src = (k_parts[h, :, n0:n0 + w] if isinstance(h, int) else
                       k_parts[bass.ds(h, 1), :, n0:n0 + w].rearrange("a r n -> (a r) n"))
                for i in range(3):
                    r0 = QROW + 3 * DH * i
                    sp.dma_start(k_op[par][r0:r0 + 3 * DH, n0:n0 + w], src).then_inc(k_loaded[par][c], 16)

            sp.wait_ge(S["const_ready"], 1)
            load_q(q_max[0], 0, qm_loaded)
            load_q(q_exp[0], 0, q_loaded)
            sp.wait_ge(qm_loaded, 16)
            load_q(q_max[1], 1, qm_loaded)
            for c in range(NC):
                last_g = min(2 * c + 2, NB)
                sp.wait_ge(S["k_hi"], last_g)
                sp.wait_ge(S["k_mid"], last_g)
                sp.wait_ge(S["k_lo"], last_g)
                n0, w = chunk(c)
                for j in range(3):
                    sp.dma_start(k_parts[:, j * DH:(j + 1) * DH, n0:n0 + w],
                                 k_split[c % 2][:, j, 0:w]).then_inc(S["k_stored"], 16)
                sp.wait_ge(S["k_stored"], 48 * (c + 1))
                load_k(0, 0, c)
            for c in range(NC):
                load_k(1, 1, c)

            sp.wait_ge(S["bt_split"], 1)
            for m in range(2):
                for j in range(3):
                    sp.dma_start(lb_parts[m, j], b_split[:, j, m * F:(m + 1) * F]).then_inc(S["b_stored"], 16)
            sp.wait_ge(S["b_stored"], 6 * 16)
            for m in range(2):
                for k, (_, j) in enumerate(TERMS):
                    sp.dma_start(lb[k * R:(k + 1) * R, m, :, :],
                                 lb_parts[m, j].rearrange("(e r) f -> r e f", r=R)).then_inc(S["b_loaded"], 16)

            def head_loads(h, par, more):
                sp.wait_ge(st_done, h * NT + 1)
                load_q(q_exp[1 - par], h + 1, q_loaded)
                if more:
                    load_q(q_max[par], h + 2, qm_loaded)
                    for c in range(NC):
                        sp.wait_ge(st_done, h * NT + min(CT * (c + 1), NT))
                        load_k(par, h + 2, c)

            def store_sums(h, par):
                sp.wait_ge(acc_free, h + 2)
                for q in range(4):
                    dst = (y_parts[q // 2, h] if isinstance(h, int) else
                           y_parts[q // 2, bass.ds(h, 1)].rearrange("a r t -> (a r) t"))
                    sp.dma_start(dst[:, (q % 2) * HALF:(q % 2 + 1) * HALF],
                                 sums[par][32 * q:32 * q + YW, :]).then_inc(y_stored[par], 16)

            with sp.Fori(0, H // 2 - 1) as i:
                head_loads(i * 2, 0, True)
                store_sums(i * 2, 0)
                head_loads(i * 2 + 1, 1, True)
                store_sums(i * 2 + 1, 1)
            head_loads(H - 2, 0, False)
            store_sums(H - 2, 0)
            store_sums(H - 1, 1)
            for i in range(2):
                sp.wait_ge(y_stored[i], 64 * (H // 2 + 1))
            for i in range(2):
                sp.dma_start(y_num[:, i, :], y_parts[i, :, 0:DH, :]).then_inc(y_loaded, 16)
            sp.dma_start(y_den, y_parts[:, :, DH, :].rearrange("i h t -> (i h) t")).then_inc(y_loaded, 16)

            for m in range(2):
                sp.wait_ge(S["la_ready"], m + 1)
                for i in range(3):
                    sp.dma_start(la_parts[m, i], la_split[m][:, i, :]).then_inc(S["la_stored"], 16)
            sp.wait_ge(S["la_stored"], 6 * 16)
            for e in range(E):
                for m in range(2):
                    for i in range(3):
                        ks = [k for k, t in enumerate(TERMS) if t[0] == i]
                        src = la_parts[m, i, e * R:(e + 1) * R, :].unsqueeze(0).to_broadcast([len(ks), R, T])
                        sp.dma_start(la[e][ks[0] * R:(ks[-1] + 1) * R, m, :], src).then_inc(la_loaded[e], 16)

            sp.wait_ge(S["out_ready"], 1)
            sp.dma_start(out[0].rearrange("(p a) d -> p a d", a=TA), x_sb[:, :, :]).then_inc(S["out_stored"], 16)
            sp.wait_ge(S["out_stored"], 16)

        @block.gpsimd
        def _(pool):
            g = nc.gpsimd
            n = 0

            def step(ins):
                nonlocal n
                n += 1
                ins.then_inc(S["pool_step"], 1)
                pool.wait_ge(S["pool_step"], n)

            def block_mask(m, w):
                step(g.memset(m[:, :], 1.0))
                step(g.affine_select(out=m[:, :], in_=m[:, :], compare_op=ALU.is_ge, fill=0.0, base=0,
                                     pattern=[[-w, m.shape[1]]], channel_multiplier=1))
                step(g.affine_select(out=m[:, :], in_=m[:, :], compare_op=ALU.is_ge, fill=0.0, base=w - 1,
                                     pattern=[[w, m.shape[1]]], channel_multiplier=-1))

            step(g.memset(ident[:, :], 0.0))
            step(g.affine_select(out=ident[:, :], in_=ident[:, :], compare_op=ALU.not_equal, fill=1.0,
                                 base=0, pattern=[[-1, 128]], channel_multiplier=1))
            g.memset(kn_t[L:L + 1, :], 1.0)
            step(g.memset(knl_t[L:L + 1, :], 1.0))
            g.tensor_copy(ident_b[:, :], ident[:, :]).then_inc(S["const_ready"], 1)
            for i in range(2):
                g.memset(q_max[i][0:QROW, :], 0.0)
                g.memset(q_exp[i][0:QROW, :], 0.0)
                step(g.memset(k_op[i][0:QROW, :], 1.0))
            block_mask(head_mask, DH)
            for e in range(E):
                g.memset(first[:, e:e + 1], float(E - e))
            block_mask(left_mask, NL)
            block_mask(expert_mask, R)
            pool.sem_inc(S["masks_ready"], 1)
            step(g.tensor_tensor(den_sel[:, :], ident[0:2 * H, 0:H], ident[0:2 * H, H:2 * H], ALU.add))
            for i in range(2):
                pool.sem_inc(y_stored[i], 64)

            pool.wait_ge(S["q_mid"], 1)
            g.tensor_tensor(q_split[:, 2, :], split_r[:, :, :].rearrange("p i n -> p (i n)"),
                            q_split[:, 1, :], ALU.subtract).then_inc(S["q_lo"], 1)
            for gi in range(NB):
                n0, w = group(gi)
                c, o = gi // 2, (gi % 2) * MB
                pool.wait_ge(S["k_mid"], gi + 1)
                g.tensor_tensor(k_split[c % 2][:, 2, o:o + w], split_r[:, gi % 2, 0:w],
                                k_split[c % 2][:, 1, o:o + w], ALU.subtract).then_inc(S["k_lo"], 1)
                if gi == 0:
                    pool.wait_ge(S["lt_ready"], 1)
                    step(g.tensor_copy(knl_rep[:, :, :],
                                       knl_t[:, :].unsqueeze(1).to_broadcast([L + 1, H, NL])))
                    pool.sem_inc(S["lrep_ready"], 1)
                if gi == 1:
                    for i in range(2):
                        step(g.memset(v_head[i][:, :, :], 0.0))
                        step(g.memset(v_head[i][:, :, DH:DH + 1], 1.0))

            def v_copy(par, h):
                g.tensor_copy(v_head[par][:, :, 0:DH], v_all[:, :, bass.ds(h * DH, DH)]).then_inc(vh_ready, 1)

            def left_max_copy(h):
                g.tensor_copy(blockmax[:, :, NB:NB + 1], left_max[:, :, bass.ds(h, 1)]).then_inc(lm_ready, 1)

            def mparts_copy(h):
                g.tensor_copy(mparts_all[:, bass.ds(h, 1), :, :].rearrange("p h a s -> p (h a s)"),
                              mparts[:, :, :].rearrange("p a s -> p (a s)")).then_inc(ms_ready, 1)

            pool.wait_ge(S["ls_ready"], 1)
            left_max_copy(0)
            pool.wait_ge(S["v_ready"], NB)
            v_copy(0, 0)

            pool.wait_ge(S["prep_ready"], 5)
            bt = b_t[:, :, :].rearrange("p m f -> p (m f)")
            step(g.tensor_copy(b_split[:, 0, :], bt))
            step(g.tensor_tensor(b_res, bt, b_split[:, 0, :], ALU.subtract))
            step(g.tensor_copy(b_split[:, 1, :], b_res))
            g.tensor_tensor(b_split[:, 2, :], b_res, b_split[:, 1, :], ALU.subtract).then_inc(S["bt_split"], 1)

            pool.wait_ge(S["prep_ready"], 6)
            for e in range(E + 1):
                if e < E:
                    if e >= 2:
                        pool.wait_ge(S["prep_ps"], 6 + e - 1)
                    g.tensor_scalar(masked[:, e % 2, :], b2_t[:, :], expert_mask[:, e:e + 1], None,
                                    ALU.mult).then_inc(S["masked_ready"], 1)
                if e >= 1:
                    pool.wait_ge(S["prep_ready"], 6 + e)
                    g.tensor_tensor(w2e[:, e - 1, :], w2e[:, e - 1, :], w_t[:, 2, :], ALU.add).then_inc(S["prep_sum"], 1)

            def after_max(h, more):
                pool.wait_ge(m_ready, h + 1)
                mparts_copy(h)
                if more:
                    left_max_copy(h + 1)

            def head(h, par, more):
                pool.wait_ge(pv_done, h * PAIRS + PVC)
                v_copy(1 - par, h + 1)
                after_max(h + 1, more)

            after_max(0, True)
            with pool.Fori(0, H // 2 - 1) as i:
                head(i * 2, 0, True)
                head(i * 2 + 1, 1, True)
            head(H - 2, 0, False)

            for n_h in range(2 * E * FC):
                u, c = n_h // FC, n_h % FC
                pool.wait_ge(S["silu_ready"], n_h + 1)
                if c == 0 and u >= 2:
                    pool.wait_ge(S["down_ps"], u - 1)
                g.tensor_tensor(act_t[:, u % 2, c, :], silu_t[:, n_h % 2, :], uv_t[:, n_h % 2, 1, :],
                                ALU.mult).then_inc(S["act_ready"], 1)

        @block.scalar
        def _(act):
            s = nc.scalar
            act.dma_start(x_sb[:, :, :], x[0].rearrange("(p a) d -> p a d", a=TA)).then_inc(S["x_in"], 16)
            act.dma_start(qw_sb[:, :], q_w).then_inc(S["qw_in"], 16)
            for i, (v, w) in enumerate(((q_b, D), (ln_g, D), (ln_b, D), (tln_g, L), (tln_b, L), (norm_w, D))):
                act.dma_start(cols[0:w, i:i + 1], v.rearrange("(p a) -> p a", a=1)).then_inc(S["cols_in"], 16)
            act.dma_start(ctx_left[:, :], ctx_in[0, NM:NK, :]).then_inc(S["ctxl_in"], 16)

            act.wait_ge(S["bn_done"], 1)
            s.activation(rx[:, 0, :], mvx[:, :, 1], ACT.Sqrt).then_inc(S["sd_done"], 1)
            act.wait_ge(S["bn_done"], 2)
            s.activation(rx[:, 1, :], mvx[:, :, 1], ACT.Sqrt).then_inc(S["sd_done"], 1)
            act.wait_ge(S["cvar_done"], 1)
            s.activation(statl[:, 2:3], statl[:, 1:2], ACT.Sqrt)
            s.activation(stat[:, 2, :], stat[:, 1, :], ACT.Sqrt).then_inc(S["csd_done"], 1)

            act.wait_ge(S["xt_ready"], 1)
            act.wait_ge(S["cols_in"], 6 * 16)
            s.activation(xn_t, SC[:, 0, :], ACT.Identity, bias=cols[:, LNB:LNB + 1],
                         scale=cols[:, LNG:LNG + 1]).then_inc(S["xn_ready"], 1)
            act.wait_ge(S["q_ready"], 1)
            s.activation(q_split[:, 0, :], q_t, ACT.Copy).then_inc(S["q_hi"], 1)
            act.wait_ge(S["q_res"], 1)
            s.activation(q_split[:, 1, :], split_r[:, :, :].rearrange("p i n -> p (i n)"), ACT.Copy).then_inc(S["q_mid"], 1)

            def kn_evac(gi):
                n0, w = group(gi)
                act.wait_ge(S["ct_ps"], gi + 1)
                s.activation(kn_t[0:L, n0:n0 + w], SCB[0:L, gi % 2, 0:w], ACT.Identity,
                             bias=cols[0:L, TLB:TLB + 1], scale=cols[0:L, TLG:TLG + 1]).then_inc(S["kn_ready"], 1)

            def k_first(gi):
                n0, w = group(gi)
                c, o = gi // 2, (gi % 2) * MB
                act.wait_ge(S["k_ps"], gi + 1)
                if c >= 2:
                    act.wait_ge(S["k_stored"], 48 * (c - 1))
                s.activation(k_split[c % 2][:, 0, o:o + w], SCB[:, 2 + gi % 2, 0:w], ACT.Copy).then_inc(S["k_hi"], 1)

            def k_second(gi):
                n0, w = group(gi)
                c, o = gi // 2, (gi % 2) * MB
                act.wait_ge(S["k_res"], gi + 1)
                s.activation(k_split[c % 2][:, 1, o:o + w], split_r[:, gi % 2, 0:w], ACT.Copy).then_inc(S["k_mid"], 1)

            for gi in range(NB + 2):
                if gi < NB:
                    kn_evac(gi)
                if gi == 1:
                    act.wait_ge(S["lt_ps"], 1)
                    s.activation(knl_t[0:L, :], AC[0:L, 0:NL], ACT.Identity, bias=cols[0:L, TLB:TLB + 1],
                                 scale=cols[0:L, TLG:TLG + 1]).then_inc(S["lt_ready"], 1)
                if 1 <= gi <= NB:
                    k_first(gi - 1)
                if gi >= 2:
                    k_second(gi - 2)

            for i in range(6):
                act.wait_ge(S["prep_ps"], i + 1)
                if i < 3:
                    s.activation(w_t[:, i, :], SCB[:, i % 4, :], ACT.Copy).then_inc(S["prep_ready"], 1)
                elif i < 5:
                    s.activation(b_t[:, i - 3, :], SCB[:, i % 4, :], ACT.Copy, scale=LORA).then_inc(S["prep_ready"], 1)
                else:
                    s.activation(b2_t[:, :], SCB[:, i % 4, 0:D], ACT.Copy)
                    s.activation(a_t[:, :, :].rearrange("p m n -> p (m n)"), SCB[:, i % 4, 128:128 + 2 * E * R], ACT.Copy)
                    s.activation(gate_t[:, :], SCB[:, i % 4, 384:384 + E], ACT.Copy).then_inc(S["prep_ready"], 1)
            for e in range(E):
                k = 6 + e
                act.wait_ge(S["prep_ps"], k + 1)
                s.activation(w2e[:, e, :], SCB[:, k % 4, :], ACT.Copy, scale=LORA).then_inc(S["prep_ready"], 1)

            def m_rows(par, h):
                act.wait_ge(mt_done, h + 1)
                s.activation(q_exp[par][0:2, :], MX[0:2, 2, :].bitcast(bf16), ACT.Copy).then_inc(mrow_ready, 1)

            act.sem_inc(exp_done, 2)
            act.sem_inc(acc_free, 1)
            m_rows(0, 0)

            def head(h, par, next_max):
                for j in range(NT):
                    if j == NT - 2 and next_max:
                        m_rows(1 - par, h + 1)
                    act.wait_ge(st_done, h * NT + j + 1)
                    act.wait_ge(pv_done, h * PAIRS + (j - PR) // 2 + 1 + PVC)
                    s.activation(probs[:, j % PR, :], SC[:, j % 2, :], ACT.Exp).then_inc(exp_done, 1)
                act.wait_ge(pv_done, (h + 1) * PAIRS + PVC)
                act.wait_ge(y_stored[par], 32 * (h - par) + 64)
                s.activation(sums[par][:, :], AC[:, :], ACT.Copy).then_inc(acc_free, 1)

            with act.Fori(0, H // 2 - 1) as i:
                head(i * 2, 0, True)
                head(i * 2 + 1, 1, True)
            head(H - 2, 0, True)
            head(H - 1, 1, False)

            act.wait_ge(S["lz_ready"], 1)
            s.activation(left_p, left_scores[:, :, :], ACT.Exp).then_inc(S["lp_ready"], 1)
            act.wait_ge(S["lpt_ps"], 1)
            s.activation(left_pt, MX[0:H * NL, 0:2, :].rearrange("p a b -> p (a b)"), ACT.Copy).then_inc(S["lpt_ready"], 1)
            act.wait_ge(S["var1_done"], 1)
            s.activation(rx[:, 0, :], mvx[:, :, 1], ACT.Sqrt).then_inc(S["sd1_done"], 1)
            act.wait_ge(S["ms_done"], 1)
            s.activation(rx[:, 1, :], gs[:, 0, :], ACT.Sqrt).then_inc(S["sd2_done"], 1)
            act.wait_ge(S["tt_ps"], 1)
            s.activation(t_t, SC[:, 0, :], ACT.Copy, scale=cols[:, NW:NW + 1]).then_inc(S["tt_ready"], 1)
            for m in range(2):
                act.wait_ge(S["la_ps"], m + 1)
                s.activation(la_split[m][:, 0, :], SC[:, 1 - m, :], ACT.Copy).then_inc(S["la_hi"], 1)
            for m in range(2):
                act.wait_ge(S["la_res_done"], m + 1)
                s.activation(la_split[m][:, 1, :], la_res[m], ACT.Copy).then_inc(S["la_mid"], 1)
            act.wait_ge(S["lg_sub"], 1)
            s.activation(gt[:, 1, :, :], gt[:, 0, :, :], ACT.Exp).then_inc(S["lg_exp"], 1)
            for n_b in range(4 * FC):
                hf, c, m = n_b // (2 * FC), n_b // 2 % FC, n_b % 2
                act.wait_ge(S["base_ps"], n_b + 1)
                s.activation(base[hf][:, c, m, :], SCB[:, n_b % 4, :], ACT.Copy).then_inc(S["base_ready"], 1)
            for n_h in range(2 * E * FC):
                act.wait_ge(S["uv_ready"], n_h + 1)
                if n_h >= 2:
                    act.wait_ge(S["act_ready"], n_h - 1)
                s.activation(silu_t[:, n_h % 2, :], uv_t[:, n_h % 2, 0, :], ACT.Silu).then_inc(S["silu_ready"], 1)

        @block.vector
        def _(dve):
            v = nc.vector
            n = 0

            def link(ins):
                nonlocal n
                n += 1
                ins.then_inc(dve_link, 1)
                dve.wait_ge(dve_link, n)

            def stats(src, eps):
                for a in range(TA):
                    v.bn_stats(bnx[:, a, :], src[:, a, :])
                link(v.memset(statl[:, 3:4], 0.0))
                for a in range(TA):
                    v.bn_aggr(mvx[:, a, :], bnx[:, a, :])
                link(v.memset(statl[:, 3:4], 0.0))
                v.tensor_scalar(mvx[:, :, 1], mvx[:, :, 1], eps, None, ALU.add).then_inc(S["bn_done"], 1)

            def normalise(dst, src, i):
                link(v.reciprocal(rx[:, i, :], rx[:, i, :]))
                for a in range(TA):
                    ins = v.tensor_scalar(dst[:, a, :], src[:, a, :], mvx[:, a, 0:1], rx[:, i, a:a + 1],
                                          ALU.subtract, ALU.mult)
                link(ins)

            dve.wait_ge(S["x_in"], 16)
            stats(x_sb, LN_EPS)
            dve.wait_ge(S["sd_done"], 1)
            normalise(z_sb, x_sb, 0)
            stats(z_sb, LN_EPS)
            dve.wait_ge(S["sd_done"], 2)
            normalise(z_sb, z_sb, 1)
            dve.sem_inc(S["xn_ready"], 1)

            dve.wait_ge(S["ctx_in_s"], 16)
            dve.wait_ge(S["ctxl_in"], 16)
            for j in range(NT):
                v.bn_stats(bn[:, j, :], ctx_sb[:, j, :])
            link(v.bn_stats(bnl[:, :], ctx_left[:, :]))
            v.bn_aggr(statl[:, 0:2], bnl[:, :])
            link(v.tensor_tensor(stat[:, 0, :], bn[:, :, 1], bn[:, :, 4], ALU.add))
            link(v.tensor_tensor(stat[:, 1, :], bn[:, :, 1], bn[:, :, 4], ALU.subtract))
            link(v.tensor_tensor(stat[:, 1, :], stat[:, 1, :], stat[:, 1, :], ALU.mult))
            link(v.tensor_tensor(stat[:, 3, :], bn[:, :, 2], bn[:, :, 5], ALU.add))
            link(v.tensor_scalar(stat[:, 3, :], stat[:, 3, :], 1.0 / L, LN_EPS, ALU.mult, ALU.add))
            link(v.tensor_scalar(statl[:, 1:2], statl[:, 1:2], LN_EPS, None, ALU.add))
            v.tensor_scalar(stat[:, 0, :], stat[:, 0, :], 0.5, None, ALU.mult)
            v.scalar_tensor_tensor(stat[:, 1, :], stat[:, 1, :], 0.25, stat[:, 3, :],
                                   ALU.mult, ALU.add).then_inc(S["cvar_done"], 1)

            dve.wait_ge(S["q_ps"], 1)
            link(v.tensor_scalar(q_t, SC[:, 1, :], cols[:, QB:QB + 1], QSCALE, ALU.add, ALU.mult))
            dve.sem_inc(S["q_ready"], 1)
            dve.wait_ge(S["q_hi"], 1)
            v.tensor_tensor(split_r[:, :, :].rearrange("p i n -> p (i n)"), q_t, q_split[:, 0, :],
                            ALU.subtract).then_inc(S["q_res"], 1)

            dve.wait_ge(S["csd_done"], 1)
            link(v.reciprocal(stat[:, 3, :], stat[:, 2, :]))
            link(v.reciprocal(statl[:, 3:4], statl[:, 2:3]))
            link(v.tensor_scalar(ctx_left[:, :], ctx_left[:, :], statl[:, 0:1], statl[:, 3:4],
                                 ALU.subtract, ALU.mult))

            def ctx_norm(gi):
                for j in range(gi * GT, min(gi * GT + GT, NT)):
                    ins = v.tensor_scalar(ctx_sb[:, j, :], ctx_sb[:, j, :], stat[:, 0, j:j + 1],
                                          stat[:, 3, j:j + 1], ALU.subtract, ALU.mult)
                ins.then_inc(S["cn_ready"], 1)

            def k_residual(gi):
                n0, w = group(gi)
                c, o = gi // 2, (gi % 2) * MB
                dve.wait_ge(S["k_hi"], gi + 1)
                if gi >= 2:
                    dve.wait_ge(S["k_lo"], gi - 1)
                else:
                    dve.wait_ge(S["q_lo"], 1)
                v.tensor_tensor(split_r[:, gi % 2, 0:w], SCB[:, 2 + gi % 2, 0:w],
                                k_split[c % 2][:, 0, o:o + w], ALU.subtract).then_inc(S["k_res"], 1)

            def v_evac(gi):
                n0, w = group(gi)
                dve.wait_ge(S["v_ps"], gi + 1)
                v.tensor_copy(v_all[:, gi * GT:gi * GT + w // 128, :].rearrange("p j d -> p (j d)"),
                              MX[:, gi % 2, 0:w]).then_inc(S["v_ready"], 1)

            ctx_norm(0)
            ctx_norm(1)
            for gi in range(NB):
                if gi + 2 < NB:
                    ctx_norm(gi + 2)
                k_residual(gi)
                v_evac(gi)
                if gi == 1:
                    dve.wait_ge(S["lk_ps"], 1)
                    dve.wait_ge(S["masks_ready"], 1)
                    link(v.tensor_copy(kl_t[:, :], AC[:, 8:8 + NL]))
                    v.tensor_tensor(kl_bd[:, :, :], kl_t[:, :].unsqueeze(1).to_broadcast([128, H, NL]),
                                    head_mask[:, :].unsqueeze(2).to_broadcast([128, H, NL]),
                                    ALU.mult).then_inc(S["lk_ready"], 1)
                    dve.wait_ge(S["lv_ps"], 1)
                    v.tensor_tensor(v_left[:, 0:D].rearrange("p (h d) -> p h d", h=H),
                                    AC[0:H * NL, 128:256].rearrange("p (h d) -> p h d", h=H),
                                    left_mask[:, :].unsqueeze(2).to_broadcast([H * NL, H, DH]), ALU.mult)
                    v.tensor_copy(v_left[:, D:D + H], left_mask[:, :]).then_inc(S["lv_ready"], 1)
                    dve.wait_ge(S["ls_ps"], 1)
                    link(v.tensor_copy(left_scores[:, :, :].rearrange("p a n -> p (a n)"), AC[:, :]))
                    v.tensor_reduce(left_max[:, :, :], left_scores[:, :, :].rearrange("p a (h n) -> p a h n", n=NL),
                                    axis=AX.X, op=ALU.max).then_inc(S["ls_ready"], 1)

            def max_block(h, b):
                kb, a = b // TA, b % TA
                w = min(MB, NM - kb * MB)
                dve.wait_ge(mb_done, h * MAXB + b + 1)
                v.tensor_reduce(blockmax[:, a, kb:kb + 1], MX[:, b % 3, 0:w], axis=AX.X,
                                op=ALU.max).then_inc(mx_done, 1)

            def max_final(h):
                dve.wait_ge(mx_done, (h + 1) * MAXB)
                dve.wait_ge(lm_ready, h + 1)
                dve.wait_ge(ms_ready, h + 1)
                v.tensor_reduce(negmax[:, :], blockmax[:, :, :], axis=AX.X, op=ALU.max,
                                negate=True).then_inc(max_link, 1)
                dve.wait_ge(max_link, h * 2 + 1)
                v.tensor_copy(mparts[:, :, 0], negmax[:, :]).then_inc(max_link, 1)
                dve.wait_ge(max_link, h * 2 + 2)
                v.tensor_tensor(mparts[:, :, 1], negmax[:, :], mparts[:, :, 0], ALU.subtract).then_inc(m_ready, 1)

            dve.sem_inc(ms_ready, 1)
            for b in range(MAXB):
                max_block(0, b)
            max_final(0)
            for b in range(AHEAD):
                max_block(1, b)

            def head(h, more):
                for b in range(AHEAD, MAXB):
                    max_block(h + 1, b)
                max_final(h + 1)
                if more:
                    for b in range(AHEAD):
                        max_block(h + 2, b)

            with dve.Fori(0, H // 2 - 1) as i:
                head(i * 2, True)
                head(i * 2 + 1, True)
            head(H - 2, False)

            dve.wait_ge(ms_ready, H + 1)
            lz = left_scores[:, :, :].rearrange("p a (h n) -> p a h n", n=NL)
            for part in range(2):
                m = mparts_all[:, :, :, part].rearrange("p h a -> p a h").unsqueeze(3)
                ins = v.tensor_tensor(lz, lz, m.to_broadcast([128, TA, H, NL]), ALU.add)
                if part == 0:
                    link(ins)
            ins.then_inc(S["lz_ready"], 1)

            for a in range(TA):
                y = SCB[:, a % 4, 0:D].rearrange("p (h d) -> p h d", d=DH)
                dve.wait_ge(S["y_ps"], a + 1)
                link(v.reciprocal(rden[:, a % 2, :], SCB[:, a % 4, D:D + H]))
                link(v.tensor_tensor(tmp[:, a, :].rearrange("p (h d) -> p h d", d=DH), y,
                                     rden[:, a % 2, :].unsqueeze(2).to_broadcast([128, H, DH]), ALU.mult))
                link(v.tensor_tensor(x_sb[:, a, :], x_sb[:, a, :], tmp[:, a, :], ALU.add))
                dve.sem_inc(S["y_ready"], 1)

            for a in range(TA):
                v.bn_stats(bnx[:, a, :], x_sb[:, a, :])
            link(v.memset(statl[:, 3:4], 0.0))
            for a in range(TA):
                v.bn_aggr(mvx[:, a, :], bnx[:, a, :])
            link(v.memset(statl[:, 3:4], 0.0))
            v.tensor_scalar(mvx[:, :, 1], mvx[:, :, 1], LN_EPS, None, ALU.add).then_inc(S["var1_done"], 1)
            dve.wait_ge(S["sd1_done"], 1)
            normalise(zt, x_sb, 0)
            link(v.tensor_tensor(tmp[:, :, :], zt, zt, ALU.mult))
            link(v.tensor_reduce(gs[:, 0, :], tmp[:, :, :], axis=AX.X, op=ALU.add))
            v.tensor_scalar(gs[:, 0, :], gs[:, 0, :], 1.0 / D, RMS_EPS, ALU.mult, ALU.add).then_inc(S["ms_done"], 1)
            dve.wait_ge(S["sd2_done"], 1)
            link(v.reciprocal(rx[:, 1, :], rx[:, 1, :]))
            v.tensor_tensor(zt, zt, rx[:, 1, :].unsqueeze(2).to_broadcast([128, TA, D]),
                            ALU.mult).then_inc(S["tn_ready"], 1)

            for m in range(2):
                dve.wait_ge(S["la_hi"], m + 1)
                v.tensor_tensor(la_res[m], SC[:, 1 - m, :], la_split[m][:, 0, :], ALU.subtract).then_inc(S["la_res_done"], 1)
            for m in range(2):
                dve.wait_ge(S["la_mid"], m + 1)
                v.tensor_tensor(la_split[m][:, 2, :], la_res[m], la_split[m][:, 1, :], ALU.subtract).then_inc(S["la_ready"], 1)

            def over_e(col):
                return col.unsqueeze(2).to_broadcast([128, TA, E])

            def e_max(dst, src):
                link(v.tensor_reduce(dst, src, axis=AX.X, op=ALU.max))

            lg = MX[:, 2, 0:TA * E].rearrange("p (a e) -> p a e", e=E)
            first_b = first[:, :].unsqueeze(1).to_broadcast([128, TA, E])
            dve.wait_ge(S["lg_ps"], 1)
            e_max(gs[:, 1, :], lg)
            v.tensor_tensor(gt[:, 0, :, :], lg, over_e(gs[:, 1, :]), ALU.subtract).then_inc(S["lg_sub"], 1)
            dve.wait_ge(S["lg_exp"], 1)
            link(v.tensor_reduce(gs[:, 2, :], gt[:, 1, :, :], axis=AX.X, op=ALU.add))
            link(v.reciprocal(gs[:, 2, :], gs[:, 2, :]))
            link(v.tensor_tensor(gt[:, 1, :, :], gt[:, 1, :, :], over_e(gs[:, 2, :]), ALU.mult))
            for top in range(2):
                pr, best = gt[:, 1 + top, :, :], gs[:, 3 + top, :]
                choice = gt[:, 3 + top, :, :]
                e_max(best, pr)
                link(v.tensor_tensor(choice, pr, over_e(best), ALU.is_equal))
                link(v.tensor_tensor(choice, choice, first_b, ALU.mult))
                e_max(gs[:, 5, :], choice)
                link(v.tensor_tensor(choice, choice, over_e(gs[:, 5, :]), ALU.is_equal))
                if top == 0:
                    link(v.scalar_tensor_tensor(gt[:, 2, :, :], choice, -2.0, pr, ALU.mult, ALU.add))
            link(v.tensor_tensor(gs[:, 6, :], gs[:, 3, :], gs[:, 4, :], ALU.add))
            link(v.reciprocal(gs[:, 6, :], gs[:, 6, :]))
            for top in range(2):
                link(v.tensor_tensor(gs[:, 3 + top, :], gs[:, 3 + top, :], gs[:, 6, :], ALU.mult))
                link(v.tensor_tensor(gt[:, 3 + top, :, :], gt[:, 3 + top, :, :], over_e(gs[:, 3 + top, :]), ALU.mult))
            link(v.tensor_tensor(gt[:, 5, :, :], gt[:, 3, :, :], gt[:, 4, :, :], ALU.add))

            def combine(u):
                e, hf = u // 2, u % 2
                dve.wait_ge(S["down_ps"], u + 1)
                for q in range(4):
                    a = hf * 4 + q
                    ins = v.scalar_tensor_tensor(x_sb[:, a, :], MX[:, u % 2, q * 128:(q + 1) * 128],
                                                 gt[:, 5, a, e:e + 1], x_sb[:, a, :], ALU.mult, ALU.add)
                link(ins)
                dve.sem_inc(S["down_used"], 1)

            for u in range(2 * E):
                for c in range(FC):
                    n_h = u * FC + c
                    dve.wait_ge(S["h_ps"], n_h + 1)
                    if n_h >= 2:
                        dve.wait_ge(S["act_ready"], n_h - 1)
                    v.tensor_tensor(uv_t[:, n_h % 2, :, :].rearrange("p m t -> p (m t)"), SC[:, n_h % 2, :],
                                    base[u % 2][:, c, :, :].rearrange("p m t -> p (m t)"),
                                    ALU.add).then_inc(S["uv_ready"], 1)
                    if c == 2 and u >= 2:
                        combine(u - 2)
            combine(2 * E - 2)
            combine(2 * E - 1)
            dve.sem_inc(S["out_ready"], 1)

        @block.tensor
        def _(pe):
            p = nc.tensor
            pe.wait_ge(S["const_ready"], 1)
            pe.wait_ge(S["xn_ready"], 1)
            for a in range(TA):
                ins = p.transpose(SC[:, 0, a * 128:(a + 1) * 128], z_sb[:, a, :], ident[:, :])
            ins.then_inc(S["xt_ready"], 1)
            pe.wait_ge(S["xn_ready"], 2)
            pe.wait_ge(S["qw_in"], 16)
            for hf in range(2):
                ins = p.matmul(SC[:, 1, hf * HALF:(hf + 1) * HALF], qw_sb[:, :],
                               xn_t[:, hf * HALF:(hf + 1) * HALF], start=True, stop=True)
            ins.then_inc(S["q_ps"], 1)

            def ctx_transpose(gi):
                pe.wait_ge(S["cn_ready"], gi + 1)
                if gi >= 2:
                    pe.wait_ge(S["kn_ready"], gi - 1)
                for j in range(gi * GT, min(gi * GT + GT, NT)):
                    o = (j - gi * GT) * 128
                    ins = p.transpose(SCB[0:L, gi % 2, o:o + 128], ctx_sb[:, j, :], ident[:, :])
                ins.then_inc(S["ct_ps"], 1)

            def k_project(gi):
                n0, w = group(gi)
                pe.wait_ge(S["kn_ready"], gi + 1)
                if gi >= 2:
                    pe.wait_ge(S["k_res"], gi - 1)
                p.matmul(SCB[:, 2 + gi % 2, 0:w], kw_sb[:, :], kn_t[:, n0:n0 + w],
                         start=True, stop=True).then_inc(S["k_ps"], 1)

            def v_project(gi):
                n0, w = group(gi)
                if gi >= 2:
                    pe.wait_ge(S["v_ready"], gi - 1)
                for o in range(0, w, 128):
                    ins = p.matmul(MX[:, gi % 2, o:o + 128], kn_t[:, n0 + o:n0 + o + 128], vw_sb[:, :],
                                   start=True, stop=True)
                ins.then_inc(S["v_ps"], 1)

            pe.wait_ge(S["q_ready"], 1)
            pe.wait_ge(S["w_in"], 4 * 16)
            pe.wait_ge(S["csd_done"], 1)
            ctx_transpose(0)
            p.transpose(AC[0:L, 0:NL], ctx_left[:, :], ident[0:NL, 0:NL]).then_inc(S["lt_ps"], 1)
            for gi in range(NB):
                if gi + 1 < NB:
                    ctx_transpose(gi + 1)
                k_project(gi)
                v_project(gi)
                if gi == 1:
                    pe.wait_ge(S["lt_ready"], 1)
                    p.matmul(AC[:, 8:8 + NL], kw_sb[:, :], knl_t[:, :], start=True, stop=True).then_inc(S["lk_ps"], 1)
                    pe.wait_ge(S["lk_ready"], 1)
                    pe.wait_ge(S["lrep_ready"], 1)
                    p.matmul(AC[0:H * NL, 128:256], knl_rep[:, :, :].rearrange("p h n -> p (h n)"), vw_sb[:, :],
                             start=True, stop=True).then_inc(S["lv_ps"], 1)
                    pe.wait_ge(S["lv_ready"], 1)
                    for a in range(TA):
                        ins = p.matmul(AC[:, a * H * NL:(a + 1) * H * NL], q_t[:, a * 128:(a + 1) * 128],
                                       kl_bd[:, :, :].rearrange("p h n -> p (h n)"), start=True, stop=True)
                    ins.then_inc(S["ls_ps"], 1)

            def prep(k):
                bank = SCB[:, k % 4, :]
                if k == 0:
                    pe.wait_ge(S["ffn_in"], 16 * 16)
                if k >= 4:
                    pe.wait_ge(S["prep_ready"], k - 3)
                else:
                    pe.wait_ge(S["kn_ready"], NB)
                    pe.wait_ge(S["k_res"], NB)
                if k < 3:
                    for c in range(FC):
                        ins = p.transpose(bank[:, c * 128:(c + 1) * 128], w_nat[:, k, c * 128:(c + 1) * 128], ident[:, :])
                elif k < 5:
                    for c in range(FC):
                        ins = p.transpose(bank[:, c * 128:(c + 1) * 128], b_nat[:, k - 3, c, :], ident[:, :])
                elif k == 5:
                    p.transpose(bank[:, 0:D], b2_nat[:, :, :].rearrange("p e r -> p (e r)"), ident[:, :])
                    for m in range(2):
                        p.transpose(bank[:, 128 * (m + 1):128 * (m + 2)], a_nat[:, m, :], ident[:, :])
                    ins = p.transpose(bank[:, 384:384 + E], gate_nat[:, :], ident[0:E, 0:E])
                else:
                    e = k - 6
                    pe.wait_ge(S["masked_ready"], e + 1)
                    for c in range(FC):
                        ins = p.matmul(bank[:, c * 128:(c + 1) * 128], a2_nat[:, c * 128:(c + 1) * 128],
                                       masked[:, e % 2, :], start=True, stop=True)
                ins.then_inc(S["prep_ps"], 1)

            def max_block(par, h, b):
                kb, a = b // TA, b % TA
                n0, w = group(kb)
                if a == 0 and kb % 2 == 0:
                    pe.wait_ge(k_loaded[par][kb // 2], (h + 2 - par) * 24)
                if b == 0:
                    pe.wait_ge(qm_loaded, (h + 1) * 16)
                if b == 2:
                    if not (isinstance(h, int) and h == 0):
                        pe.wait_ge(mrow_ready, h)
                elif not (isinstance(h, int) and h == 0 and b < 2):
                    pe.wait_ge(mx_done, h * MAXB + (b - 2 if b > 2 else b - 1))
                p.matmul(MX[:, b % 3, 0:w], q_max[par][0:KR, a * 128:(a + 1) * 128],
                         k_op[par][0:KR, n0:n0 + w], start=True, stop=True).then_inc(mb_done, 1)

            def max_transpose(h):
                pe.wait_ge(m_ready, h + 1)
                for a in range(TA):
                    ins = p.transpose(MX[0:2, 2, :].bitcast(bf16)[:, a * 128:(a + 1) * 128], mparts[:, a, :],
                                      ident_b[:, :])
                ins.then_inc(mt_done, 1)

            pe.wait_ge(S["v_ready"], NB)
            steps = 6 + E
            done = 0
            for b in range(MAXB):
                max_block(0, 0, b)
                if b % 3 == 2 and done < steps:
                    prep(done)
                    done += 1
            while done < steps:
                prep(done)
                done += 1
            max_transpose(0)
            for b in range(AHEAD):
                max_block(1, 1, b)
            pe.wait_ge(S["prep_ready"], steps)
            pe.wait_ge(S["ls_ready"], 1)
            pe.sem_inc(pv_done, PVC)

            def scores(par, h, j):
                if j == 0:
                    pe.wait_ge(mrow_ready, h + 1)
                    pe.wait_ge(q_loaded, (h + 1) * 16)
                pe.wait_ge(exp_done, h * NT + j + 1)
                for hf in range(2):
                    ins = p.matmul(SC[:, j % 2, hf * HALF:(hf + 1) * HALF], k_op[par][0:KR, j * 128:(j + 1) * 128],
                                   q_exp[par][0:KR, hf * HALF:(hf + 1) * HALF], start=True, stop=True)
                ins.then_inc(st_done, 1)

            def v_products(par, h, k):
                if k == 0:
                    pe.wait_ge(vh_ready, h + 1)
                    pe.wait_ge(acc_free, h + 1)
                pe.wait_ge(exp_done, h * NT + 2 * k + 2 + 2)
                for q in range(4):
                    j, hf = 2 * k + q // 2, q % 2
                    ins = p.matmul(AC[32 * q:32 * q + VW, :], v_head[par][:, j, :],
                                   probs[:, j % PR, hf * HALF:(hf + 1) * HALF],
                                   start=(k == 0), stop=(k == PAIRS - 1))
                ins.then_inc(pv_done, 1)

            def head(par, h, next_max, more):
                stream = []
                rest = lambda: None
                if next_max:
                    stream += [lambda b=b: max_block(1 - par, h + 1, b) for b in range(AHEAD, MAXB)]
                    if more:
                        stream += [lambda b=b: max_block(par, h + 2, b) for b in range(2)]
                        stream += [lambda: max_transpose(h + 1), rest]
                        stream += [lambda b=b: max_block(par, h + 2, b) for b in range(2, AHEAD)]
                    else:
                        stream += [lambda: max_transpose(h + 1)]
                at = 0
                def some(slot):
                    nonlocal at
                    upto = -(-len(stream) * (slot + 1) // (4 * PAIRS))
                    while at < upto:
                        stream[at]()
                        at += 1
                for k in range(PAIRS):
                    scores(par, h, 2 * k)
                    some(4 * k)
                    scores(par, h, 2 * k + 1)
                    some(4 * k + 1)
                    if k >= 1:
                        v_products(par, h, k - 1)
                    some(4 * k + 3)
                v_products(par, h, PAIRS - 1)

            with pe.Fori(0, H // 2 - 1) as i:
                head(0, i * 2, True, True)
                head(1, i * 2 + 1, True, True)
            head(0, H - 2, True, False)
            head(1, H - 1, False, False)

            pe.wait_ge(S["lp_ready"], 1)
            for a in range(TA):
                ins = p.transpose(MX[0:H * NL, a // 4, (a % 4) * 128:(a % 4 + 1) * 128], left_p[:, a, :], ident[:, :])
            ins.then_inc(S["lpt_ps"], 1)
            pe.wait_ge(S["lpt_ready"], 1)
            pe.wait_ge(exp_done, H * NT + 2)
            for a in range(TA):
                if a >= 4:
                    pe.wait_ge(S["y_ready"], a - 3)
                p.matmul(SCB[:, a % 4, 0:H * YW], left_pt[:, a * 128:(a + 1) * 128],
                         v_left[:, :], start=True, stop=False, skip_group_check=True)
                if a == 0:
                    pe.wait_ge(y_loaded, 48)
                for i in range(2):
                    p.matmul(SCB[:, a % 4, 0:D], y_num[:, i, a * 128:(a + 1) * 128], ident[:, :],
                             start=False, stop=False, skip_group_check=True)
                p.matmul(SCB[:, a % 4, D:D + H], y_den[:, a * 128:(a + 1) * 128], den_sel[:, :],
                         start=False, stop=True, skip_group_check=True).then_inc(S["y_ps"], 1)

            pe.wait_ge(S["tn_ready"], 1)
            for a in range(TA):
                ins = p.transpose(SC[:, 0, a * 128:(a + 1) * 128], zt[:, a, :], ident[:, :])
            ins.then_inc(S["tt_ps"], 1)
            pe.wait_ge(S["tt_ready"], 1)
            for m in range(2):
                for hf in range(2):
                    ins = p.matmul(SC[:, 1 - m, hf * HALF:(hf + 1) * HALF], a_t[:, m, :],
                                   t_t[:, hf * HALF:(hf + 1) * HALF], start=True, stop=True)
                ins.then_inc(S["la_ps"], 1)
            for a in range(TA):
                ins = p.matmul(MX[:, 2, a * E:(a + 1) * E], t_t[:, a * 128:(a + 1) * 128], gate_t[:, :],
                               start=True, stop=True)
            ins.then_inc(S["lg_ps"], 1)

            pe.wait_ge(S["la_res_done"], 2)
            for n_b in range(4 * FC):
                hf, c, m = n_b // (2 * FC), n_b // 2 % FC, n_b % 2
                if n_b >= 4:
                    pe.wait_ge(S["base_ready"], n_b - 3)
                p.matmul(SCB[:, n_b % 4, :], w_t[:, m, c * 128:(c + 1) * 128],
                         t_t[:, hf * HALF:(hf + 1) * HALF], start=True, stop=True).then_inc(S["base_ps"], 1)
            pe.wait_ge(S["base_ready"], 4 * FC)
            pe.wait_ge(S["b_loaded"], 16 * 2 * len(TERMS))

            def up(u, c):
                e, hf = u // 2, u % 2
                n_h = u * FC + c
                if n_h >= 2:
                    pe.wait_ge(S["uv_ready"], n_h - 1)
                if hf == 0 and c == 0:
                    pe.wait_ge(la_loaded[e], 6 * 16)
                for m in range(2):
                    ins = p.matmul(SC[:, n_h % 2, m * HALF:(m + 1) * HALF], lb[:, m, e, c * 128:(c + 1) * 128],
                                   la[e][:, m, hf * HALF:(hf + 1) * HALF], start=True, stop=True)
                ins.then_inc(S["h_ps"], 1)

            def down(u, q):
                e = u // 2
                if q == 0:
                    pe.wait_ge(S["act_ready"], (u + 1) * FC)
                    if u >= 2:
                        pe.wait_ge(S["down_used"], u - 1)
                for c in range(FC):
                    ins = p.matmul(MX[:, u % 2, q * 128:(q + 1) * 128], act_t[:, u % 2, c, q * 128:(q + 1) * 128],
                                   w2e[:, e, c * 128:(c + 1) * 128], start=(c == 0), stop=(c == FC - 1))
                if q == 3:
                    ins.then_inc(S["down_ps"], 1)

            pe.wait_ge(S["prep_sum"], E)
            for i in range(2 * E * FC + DOWN_LAG):
                if i < 2 * E * FC:
                    up(i // FC, i % FC)
                if i >= DOWN_LAG:
                    down((i - DOWN_LAG) // 4, (i - DOWN_LAG) % 4)


_INS = ['x', 'ctx_768', 'L0_xattn_q_w', 'L0_xattn_q_b', 'L0_xattn_k_w', 'L0_xattn_k_b', 'L0_xattn_v_w',
        'L0_xattn_v_b', 'L0_xattn_ln_g', 'L0_xattn_ln_b', 'L0_xattn_tln_g', 'L0_xattn_tln_b', 'L0_ffn_norm_w',
        'L0_ffn_w1', 'L0_ffn_w3', 'L0_ffn_w2', 'L0_ffn_gate_w', 'L0_ffn_a1', 'L0_ffn_b1', 'L0_ffn_a3',
        'L0_ffn_b3', 'L0_ffn_a2', 'L0_ffn_b2']


def kernel(**inputs):
    import concourse.bacc as _bacc
    from concourse.bass_utils import run_bass_kernel_spmd as _run

    nc = _bacc.Bacc("TRN2", target_bir_lowering=False, num_devices=1)
    arrays, args = {}, []
    for name in _INS:
        a = np.ascontiguousarray(inputs[name])
        arrays[f"in_{name}"] = a
        args.append(nc.dram_tensor(f"in_{name}", a.shape, mybir.dt.from_np(a.dtype), kind="ExternalInput").ap())
    out = nc.dram_tensor("out_0", tuple(inputs["x"].shape), mybir.dt.float32, kind="ExternalOutput").ap()
    xattn_ffn(nc, *args, out)
    r = _run(nc, [arrays], core_ids=[0])
    return r.results[0]["out_0"]
```

```python
import numpy as np

import concourse.bass as bass
from concourse import mybir
from contextlib import ExitStack


def xattn_ffn(nc, x, ctx_in, q_w, q_b, k_w, k_b, v_w, v_b, ln_g, ln_b, tln_g, tln_b,
              norm_w, w1, w3, w2, gate_w, a1, b1, a3, b3, a2, b2, out):
    fp32 = mybir.dt.float32
    bf16 = mybir.dt.bfloat16
    ALU = mybir.AluOpType
    ACT = mybir.ActivationFunctionType
    AX = mybir.AxisListType

    T, D = x.shape[1], x.shape[2]
    NK, L = ctx_in.shape[1], ctx_in.shape[2]
    H = 16
    DH = D // H
    TA = T // 128
    NT = NK // 128
    NM = NT * 128
    NL = NK - NM
    HALF = T // 2
    F = w1.shape[0]
    FC = F // 128
    E, R = a1.shape[0], a1.shape[1]
    LN_EPS, RMS_EPS, LORA = 1e-5, 1e-6, 2.0
    QSCALE = float(1.0 / np.sqrt(np.float32(DH)))

    QROW = 32
    KR = QROW + 9 * DH
    VW = 32
    YW = DH + 1
    CT = 8
    CW = CT * 128
    NC = -(-NT // CT)
    MB = 512
    GT = MB // 128
    NB = -(-NM // MB)
    MAXB = NB * TA
    AHEAD = 2 * TA
    ROWS_AT = NT - 6
    LEFT_AT = 2
    PR = 5
    PAIRS = NT // 2
    LAG = 3
    MLAG = 3
    EARLY = 4
    TE = EARLY * GT
    KNR = 4
    WSTEPS = 6 + E
    TERMS = [(i, j) for i in range(3) for j in range(3)][:128 // R]
    DOWN_LAG = FC + 2
    HR = 3

    def mx_bank(b):
        return b % 2 if b < 4 else (b - 2) % 3

    def chunk(c):
        return c * CW, min(CW, NM - c * CW)

    def group(g):
        return g * MB, min(MB, NM - g * MB)

    q_parts = nc.dram_tensor("q_parts", (H, 9 * DH, T), bf16, kind="Internal").ap()
    y_parts = nc.dram_tensor("y_parts", (2, H, YW, T), fp32, kind="Internal").ap()
    la_parts = nc.dram_tensor("la_parts", (2, 3, E * R, T), bf16, kind="Internal").ap()
    lb_parts = nc.dram_tensor("lb_parts", (2, 3, E * R, F), bf16, kind="Internal").ap()
    k_parts = nc.dram_tensor("k_parts", (H, 3 * DH, NM), bf16, kind="Internal").ap()

    ctx = ExitStack()
    with ctx:
        def sb(name, shape, dt=fp32):
            return ctx.enter_context(nc.sbuf_tensor(name, shape, dt))

        def pb(name, shape, dt=fp32):
            return ctx.enter_context(nc.psum_tensor(name, shape, dt))

        def sem(name):
            return ctx.enter_context(nc.semaphore(name))

        x_sb = sb("x_sb", [128, TA, D])
        k_op = [sb(f"k_op{i}", [128, NM], bf16) for i in range(2)]
        q_exp = [sb(f"q_exp{i}", [128, T], bf16) for i in range(2)]
        q_max = [sb(f"q_max{i}", [128, T], bf16) for i in range(2)]
        v_all = sb("v_all", [128, NT, D])
        v_head = [sb(f"v_head{i}", [128, NT, VW]) for i in range(2)]
        probs = sb("probs", [128, PR, T])
        blockmax = sb("blockmax", [128, TA, NB + 1])
        negmax = sb("negmax", [128, TA])
        mparts = sb("mparts", [128, TA, 2], bf16)
        mparts_all = sb("mparts_all", [128, H, TA, 2], bf16)
        left_scores = sb("left_scores", [128, TA, H * NL])
        left_max = sb("left_max", [128, TA, H])
        v_left = sb("v_left", [H * NL, H * YW])
        ident = sb("ident", [128, 128])
        ident_b = sb("ident_b", [128, 128], bf16)
        sum_sel = sb("sum_sel", [128, 2, YW])
        sums = [sb(f"sums{i}", [128, HALF]) for i in range(2)]

        space1 = sb("space1", [128, 3 * E * F])
        ctx_sb = space1[:, 0:NT * L].rearrange("p (j l) -> p j l", l=L)
        kn_t = space1[0:L + 1, NT * L:NT * L + KNR * MB]
        kn_t = kn_t.rearrange("p (g n) -> p g n", g=KNR)
        q_t = space1[:, NT * L + KNR * MB:NT * L + KNR * MB + T]
        lb = space1[:, 0:E * F].bitcast(bf16).rearrange("p (m e f) -> p m e f", m=2, e=E)
        b_split = space1[:, E * F:E * F + 3 * F].bitcast(bf16).rearrange("p (j n) -> p j n", j=3)
        b_res = space1[:, E * F + 3 * F:E * F + 5 * F]
        w2e = space1[:, 2 * E * F:3 * E * F].rearrange("p (e f) -> p e f", e=E)
        space2 = sb("space2", [128, 7680])
        y_num = space2[:, 0:2 * T].rearrange("p (i t) -> p i t", i=2)
        y_den = space2[0:H - 1, 2 * T:4 * T].rearrange("p (i t) -> p i t", i=2)
        la_split = [space2[:, 1536 * i:1536 * (i + 1)].bitcast(bf16).rearrange("p (s n) -> p s n", s=3)
                    for i in range(2)]
        base = [w.rearrange("p (c m t) -> p c m t", c=FC, m=2)
                for w in (space1[:, E * F:2 * E * F], space2[:, 3 * T:3 * T + E * F])]
        k_split = [space2[:, 1536 * i:1536 * (i + 1)].bitcast(bf16).rearrange("p (s n) -> p s n", s=3)
                   for i in range(2)]
        q_split = space2[:, 3072:4608].bitcast(bf16).rearrange("p (s n) -> p s n", s=3)
        split_r = space2[:, 4608:5632].rearrange("p (i n) -> p i n", i=2)
        z_sb = space2[:, 5632:6656].rearrange("p (a d) -> p a d", d=D)
        xn_t = space2[:, 6656:7680]

        ctx_left = sb("ctx_left", [NL, L])
        bn = sb("bn", [128, NT, 6])
        stat = sb("stat", [128, 4, NT])
        bnl = sb("bnl", [NL, 6])
        statl = sb("statl", [NL, 4])
        bnx = sb("bnx", [128, TA, 6])
        mvx = sb("mvx", [128, TA, 2])
        rx = sb("rx", [128, 2, TA])
        knl_t = sb("knl_t", [L + 1, NL])
        knl_rep = sb("knl_rep", [L + 1, H, NL])
        kw_sb = sb("kw_sb", [L + 1, D])
        vw_sb = sb("vw_sb", [L + 1, D])
        qw_sb = sb("qw_sb", [D, D])
        cols = sb("cols", [128, 8])
        kl_t = sb("kl_t", [128, NL])
        kl_bd = sb("kl_bd", [128, H, NL])
        head_mask = sb("head_mask", [128, H])
        left_mask = sb("left_mask", [H * NL, H])
        expert_mask = sb("expert_mask", [128, E])
        QB, LNG, LNB, TLG, TLB, NW = range(6)

        probs_w = probs[:, :, :].rearrange("p r t -> p (r t)")
        w_nat = probs_w[:, 0:3 * F].rearrange("p (i f) -> p i f", i=3)
        b_nat = probs_w[:, 3 * F:5 * F].rearrange("p (i c n) -> p i c n", i=2, c=FC)
        b2_nat = sb("b2_nat", [128, E, R])
        a_nat = sb("a_nat", [128, 2, D])
        a2_nat = sb("a2_nat", [128, F])
        gate_nat = sb("gate_nat", [E, D])
        w_t = sb("w_t", [128, 3, F])
        b_t = sb("b_t", [128, 2, F])
        b2_t = sb("b2_t", [128, D])
        gate_t = sb("gate_t", [D, E])
        a_t = sb("a_t", [D, 2, E * R])
        masked = sb("masked", [128, 2, D])

        t_t = probs_w[:, 0:T]
        act_t = probs_w[:, T:T + 2 * FC * HALF].rearrange("p (i c t) -> p i c t", i=2, c=FC)
        op0_w, op1_w = k_op[0][:, :].bitcast(fp32), k_op[1][:, :].bitcast(fp32)
        left_p = op0_w[:, 0:TA * H * NL].rearrange("p (a n) -> p a n", a=TA)
        left_pt = op0_w[0:H * NL, 512:512 + T]
        tmp = op0_w[:, 1536:1536 + T].rearrange("p (a d) -> p a d", a=TA)
        zt = op1_w[:, 0:T].rearrange("p (a d) -> p a d", a=TA)
        la_res = [op1_w[:, T:2 * T], op1_w[:, 0:T]]
        uv_t = op0_w[:, 0:HR * T].rearrange("p (i m t) -> p i m t", i=HR, m=2)
        v_flat = v_all[:, :, :].rearrange("p j d -> p (j d)")
        la = [w.bitcast(bf16).rearrange("p (m t) -> p m t", m=2)
              for w in [v_flat[:, e * T:(e + 1) * T] for e in range(E - 2)] +
              [v_head[i][:, :, :].rearrange("p j w -> p (j w)")[:, 0:T] for i in range(2)]]
        gt = op1_w[:, T + 2 * HALF:T + 2 * HALF + 8 * TA * E].rearrange("p (i a e) -> p i a e", i=8, a=TA)
        gs = sb("gs", [128, 8, TA])
        rden = sb("rden", [128, TA, H])
        first = sb("first", [128, E])

        SC = pb("SC", [128, 2, T])
        MX = pb("MX", [128, 3, MB])
        AC = pb("AC", [128, HALF])
        SCB = SC[:, :, :].rearrange("p a (b c) -> p (a b) c", c=MB)

        names = ("const_ready masks_ready pool_step x_in w_in qw_in cols_in ctx_in_s ctxl_in ffn_in "
                 "z_ready rows_ready masks0_ready bn_done sd_done xt_ready xn_ready q_ps q_ready q_hi q_mid q_res q_lo "
                 "k_copied cvar_done csd_done cstat_ready cn_ready cn_act_ready ct_ps kn_ready k_ps k_hi k_res k_mid k_lo "
                 "v_ps v_ready k_stored q_stored lt_ps lt_ready lk_ps lk_ready lv_ps lv_ready lrep_ready "
                 "ls_ps ls_ready prep_ps prep_ready prep_sum masked_ready "
                 "lz_ready lp_ready lpt_ps lpt_ready y_ps y_sum var1_done sd1_done zt_ready sq_done ms_done sd2_done "
                 "tn_ready tt_ps tt_ready lg_ps lg_sub lg_exp h_ps silu_ready act_ready "
                 "bt_split b_stored b_loaded la_ps la_hi la_mid la_res_done la_ready la_stored base_ps base_ready uv_ready "
                 "down_ps down_used out_ready out_stored").split()
        S = {n: sem(n) for n in names}
        k_loaded = [[sem(f"k_loaded{i}_{c}") for c in range(NC)] for i in range(2)]
        y_stored = [sem(f"y_stored{i}") for i in range(2)]
        kg_loaded = [sem(f"kg_loaded{i}") for i in range(2)]
        y_loaded = sem("y_loaded")
        la_loaded = [sem(f"la_loaded{e}") for e in range(E)]
        q_loaded = sem("q_loaded")
        qm_loaded = sem("qm_loaded")
        st_done = sem("st_done")
        exp_done = sem("exp_done")
        pv_done = sem("pv_done")
        acc_free = sem("acc_free")
        mb_done = sem("mb_done")
        mx_done = sem("mx_done")
        m_ready = sem("m_ready")
        dve_link = sem("dve_link")
        max_link = sem("max_link")
        mt_done = sem("mt_done")
        mrow_ready = sem("mrow_ready")
        vh_ready = sem("vh_ready")
        lm_ready = sem("lm_ready")
        ms_ready = sem("ms_ready")
        PVC = 3

        def y_tile(a, c0, c1):
            return MX[:, a // 3, (a % 3) * H * YW + c0:(a % 3) * H * YW + c1]

        block = ctx.enter_context(nc.Block())

        @block.sync
        def _(sp):
            cv = ctx_in[0, 0:NM, :].rearrange("(p j) l -> p j l", p=128)
            sp.dma_start(x_sb[:, :, :], x[0].rearrange("(p a) d -> p a d", a=TA)).then_inc(S["x_in"], 16)
            sp.dma_start(ctx_sb[:, 0:TE, :], cv[:, 0:TE, :]).then_inc(S["ctx_in_s"], 16)
            sp.dma_start(kw_sb[0:L, :], k_w).then_inc(S["w_in"], 16)
            sp.dma_start(kw_sb[L:L + 1, :], k_b.rearrange("(a n) -> a n", a=1)).then_inc(S["w_in"], 16)
            sp.dma_start(vw_sb[0:L, :], v_w).then_inc(S["w_in"], 16)
            sp.dma_start(vw_sb[L:L + 1, :], v_b.rearrange("(a n) -> a n", a=1)).then_inc(S["w_in"], 16)
            sp.wait_ge(S["ctx_in_s"], 16)
            sp.dma_start(ctx_sb[:, TE:NT, :], cv[:, TE:NT, :]).then_inc(S["ctx_in_s"], 16)
            for i, w in enumerate((w1, w3)):
                sp.dma_start(w_nat[:, i, :].rearrange("p (c d) -> p c d", c=FC),
                             w.rearrange("(c p) d -> p c d", p=128)).then_inc(S["ffn_in"], 16)
            sp.dma_start(w_nat[:, 2, :], w2).then_inc(S["ffn_in"], 16)
            for i, b in enumerate((b1, b3)):
                for c in range(FC):
                    sp.dma_start(b_nat[:, i, c, :].rearrange("p (e r) -> p e r", e=E),
                                 b[:, c * 128:(c + 1) * 128, :].rearrange("e p r -> p e r")).then_inc(S["ffn_in"], 16)
            sp.dma_start(b2_nat[:, :, :], b2.rearrange("e d r -> d e r")).then_inc(S["ffn_in"], 16)
            for i, a in enumerate((a1, a3)):
                sp.dma_start(a_nat[:, i, :], a.rearrange("e r d -> (e r) d")).then_inc(S["ffn_in"], 16)
            sp.dma_start(a2_nat[:, :], a2.rearrange("e r f -> (e r) f")).then_inc(S["ffn_in"], 16)
            sp.dma_start(gate_nat[:, :], gate_w).then_inc(S["ffn_in"], 16)

            for i, part in enumerate(("q_hi", "q_mid", "q_lo")):
                sp.wait_ge(S[part], 1)
                for j in range(3):
                    r0 = (3 * i + j) * DH
                    sp.dma_start(q_parts[:, r0:r0 + DH, :], q_split[:, i, :]).then_inc(S["q_stored"], 16)

            def load_q(dst, h, done):
                sp.dma_start(dst[QROW:KR, :], q_parts[h, :, :] if isinstance(h, int) else
                             q_parts[bass.ds(h, 1), :, :].rearrange("a r t -> (a r) t")).then_inc(done, 16)

            def load_k(par, h, c):
                n0, w = chunk(c)
                src = (k_parts[h, :, n0:n0 + w] if isinstance(h, int) else
                       k_parts[bass.ds(h, 1), :, n0:n0 + w].rearrange("a r n -> (a r) n"))
                for i in range(3):
                    r0 = QROW + 3 * DH * i
                    sp.dma_start(k_op[par][r0:r0 + 3 * DH, n0:n0 + w], src).then_inc(k_loaded[par][c], 16)

            def store_k(gi):
                n0, w = group(gi)
                c, o = gi // 2, (gi % 2) * MB
                sp.wait_ge(S["k_lo"], gi + 1)
                sp.wait_ge(S["k_mid"], gi + 1)
                sp.wait_ge(S["k_hi"], gi + 1)
                for j in range(3):
                    sp.dma_start(k_parts[:, j * DH:(j + 1) * DH, n0:n0 + w],
                                 k_split[c % 2][:, j, o:o + w]).then_inc(S["k_stored"], 16)

            store_k(0)
            sp.wait_ge(S["q_stored"], 9 * 16)
            load_q(q_max[0], 0, qm_loaded)
            load_q(q_exp[0], 0, q_loaded)
            for gi in range(NB):
                n0, w = group(gi)
                if gi >= 1:
                    store_k(gi)
                sp.wait_ge(S["k_stored"], 48 * (gi + 1))
                if gi >= 2:
                    sp.wait_ge(kg_loaded[gi % 2], 48 * (gi // 2))
                for i in range(3):
                    r0 = QROW + 3 * DH * i
                    sp.dma_start(k_op[0][r0:r0 + 3 * DH, n0:n0 + w],
                                 k_parts[0, :, n0:n0 + w]).then_inc(kg_loaded[gi % 2], 16)
                if gi == 2:
                    sp.wait_ge(qm_loaded, 16)
                    load_q(q_max[1], 1, qm_loaded)
            for c in range(NC):
                load_k(1, 1, c)

            def head_loads(h, par, more):
                sp.wait_ge(st_done, h * NT + 1)
                load_q(q_exp[1 - par], h + 1, q_loaded)
                if more:
                    load_q(q_max[par], h + 2, qm_loaded)
                    for c in range(NC):
                        sp.wait_ge(st_done, h * NT + min(CT * (c + 1), NT))
                        load_k(par, h + 2, c)

            def store_sums(h, par):
                sp.wait_ge(acc_free, h + 2)
                for q in range(4):
                    dst = (y_parts[q // 2, h] if isinstance(h, int) else
                           y_parts[q // 2, bass.ds(h, 1)].rearrange("a r t -> (a r) t"))
                    sp.dma_start(dst[:, (q % 2) * HALF:(q % 2 + 1) * HALF],
                                 sums[par][32 * q:32 * q + YW, :]).then_inc(y_stored[par], 16)

            with sp.Fori(0, H // 2 - 1) as i:
                head_loads(i * 2, 0, True)
                store_sums(i * 2, 0)
                head_loads(i * 2 + 1, 1, True)
                store_sums(i * 2 + 1, 1)
            head_loads(H - 2, 0, False)

            sp.wait_ge(S["bt_split"], 1)
            for m in range(2):
                for j in range(3):
                    sp.dma_start(lb_parts[m, j], b_split[:, j, m * F:(m + 1) * F]).then_inc(S["b_stored"], 16)
            sp.wait_ge(S["b_stored"], 6 * 16)
            for m in range(2):
                for k, (_, j) in enumerate(TERMS):
                    sp.dma_start(lb[k * R:(k + 1) * R, m, :, :],
                                 lb_parts[m, j].rearrange("(e r) f -> r e f", r=R)).then_inc(S["b_loaded"], 16)

            store_sums(H - 2, 0)
            sp.wait_ge(y_stored[0], 64 * (H // 2 + 1))
            sp.wait_ge(y_stored[1], 64 * (H // 2))
            for i in range(2):
                sp.dma_start(y_num[0:D - DH, i, :], y_parts[i, 0:H - 1, 0:DH, :]).then_inc(y_loaded, 16)
            sp.dma_start(y_den, y_parts[:, 0:H - 1, DH, :].rearrange("i h t -> h i t")).then_inc(y_loaded, 16)

            for i, part in enumerate(("la_hi", "la_mid", "la_ready")):
                for m in range(2):
                    sp.wait_ge(S[part], m + 1)
                    sp.dma_start(la_parts[m, i], la_split[m][:, i, :]).then_inc(S["la_stored"], 16)
            sp.wait_ge(S["la_stored"], 6 * 16)
            for e in range(E):
                for m in range(2):
                    for i in range(3):
                        ks = [k for k, t in enumerate(TERMS) if t[0] == i]
                        src = la_parts[m, i, e * R:(e + 1) * R, :].unsqueeze(0).to_broadcast([len(ks), R, T])
                        sp.dma_start(la[e][ks[0] * R:(ks[-1] + 1) * R, m, :], src).then_inc(la_loaded[e], 16)

            sp.wait_ge(S["out_ready"], 1)
            sp.dma_start(out[0].rearrange("(p a) d -> p a d", a=TA), x_sb[:, :, :]).then_inc(S["out_stored"], 16)
            sp.wait_ge(S["out_stored"], 16)

        @block.gpsimd
        def _(pool):
            g = nc.gpsimd
            n = 0

            def step(ins):
                nonlocal n
                n += 1
                ins.then_inc(S["pool_step"], 1)
                pool.wait_ge(S["pool_step"], n)

            def block_mask(m, w):
                step(g.memset(m[:, :], 1.0))
                step(g.affine_select(out=m[:, :], in_=m[:, :], compare_op=ALU.is_ge, fill=0.0, base=0,
                                     pattern=[[-w, m.shape[1]]], channel_multiplier=1))
                step(g.affine_select(out=m[:, :], in_=m[:, :], compare_op=ALU.is_ge, fill=0.0, base=w - 1,
                                     pattern=[[w, m.shape[1]]], channel_multiplier=-1))

            step(g.memset(ident[:, :], 0.0))
            step(g.affine_select(out=ident[:, :], in_=ident[:, :], compare_op=ALU.not_equal, fill=1.0,
                                 base=0, pattern=[[-1, 128]], channel_multiplier=1))
            g.memset(kn_t[L:L + 1, :, :], 1.0)
            step(g.memset(knl_t[L:L + 1, :], 1.0))
            step(g.tensor_copy(ident_b[:, :], ident[:, :]))
            pool.sem_inc(S["const_ready"], 1)
            for i in range(2):
                g.memset(q_max[i][0:QROW, :], 0.0)
                g.memset(q_exp[i][0:QROW, :], 0.0)
                step(g.memset(k_op[i][0:QROW, :], 1.0))
                pool.sem_inc(S["rows_ready"], 1)
                if i == 0:
                    block_mask(head_mask, DH)
                    block_mask(left_mask, NL)
                    pool.sem_inc(S["masks0_ready"], 1)
            for e in range(E):
                g.memset(first[:, e:e + 1], float(E - e))
            block_mask(expert_mask, R)
            pool.sem_inc(S["masks_ready"], 1)
            for i in range(2):
                step(g.tensor_tensor(sum_sel[:, i, :], ident[:, 32 * i:32 * i + YW],
                                     ident[:, 64 + 32 * i:64 + 32 * i + YW], ALU.add))
            for i in range(2):
                pool.sem_inc(y_stored[i], 64)

            pool.wait_ge(S["lt_ready"], 1)
            g.tensor_copy(knl_rep[:, :, :],
                          knl_t[:, :].unsqueeze(1).to_broadcast([L + 1, H, NL])).then_inc(S["lrep_ready"], 1)
            pool.wait_ge(S["q_mid"], 1)
            g.tensor_tensor(q_split[:, 2, :], split_r[:, :, :].rearrange("p i n -> p (i n)"),
                            q_split[:, 1, :], ALU.subtract).then_inc(S["q_lo"], 1)

            def v_copy(par, h):
                g.tensor_copy(v_head[par][:, :, 0:DH], v_all[:, :, bass.ds(h * DH, DH)]).then_inc(vh_ready, 1)

            def left_max_copy(h):
                g.tensor_copy(blockmax[:, :, NB:NB + 1], left_max[:, :, bass.ds(h, 1)]).then_inc(lm_ready, 1)

            def mparts_copy(h):
                g.tensor_copy(mparts_all[:, bass.ds(h, 1), :, :].rearrange("p h a s -> p (h a s)"),
                              mparts[:, :, :].rearrange("p a s -> p (a s)")).then_inc(ms_ready, 1)

            for st in range(1, WSTEPS + 2 + LAG):
                gi = st - 1
                if gi < NB:
                    n0, w = group(gi)
                    c, o = gi // 2, (gi % 2) * MB
                    pool.wait_ge(S["k_hi"], gi + 1)
                    pool.wait_ge(S["k_copied"], gi + 1)
                    g.tensor_tensor(split_r[:, gi % 2, 0:w], split_r[:, gi % 2, 0:w],
                                    k_split[c % 2][:, 0, o:o + w], ALU.subtract).then_inc(S["k_res"], 1)
                if gi < NB:
                    pool.wait_ge(S["k_mid"], gi + 1)
                    g.tensor_tensor(k_split[c % 2][:, 2, o:o + w], split_r[:, gi % 2, 0:w],
                                    k_split[c % 2][:, 1, o:o + w], ALU.subtract).then_inc(S["k_lo"], 1)
                if st in (4, 5):
                    step(g.memset(v_head[st - 4][:, :, :], 0.0))
                    step(g.memset(v_head[st - 4][:, :, DH:DH + 1], 1.0))
                if st == 6:
                    pool.wait_ge(S["ls_ready"], 1)
                    left_max_copy(0)
                e = st - (6 + LAG)
                if 0 <= e < E:
                    if e == 0:
                        pool.wait_ge(S["prep_ready"], 6)
                    if e >= 2:
                        pool.wait_ge(S["prep_ps"], 6 + e - 1)
                    g.tensor_scalar(masked[:, e % 2, :], b2_t[:, :], expert_mask[:, e:e + 1], None,
                                    ALU.mult).then_inc(S["masked_ready"], 1)
                e = st - (6 + LAG + 1)
                if 0 <= e < E:
                    pool.wait_ge(S["prep_ready"], 6 + e + 1)
                    g.tensor_tensor(w2e[:, e, :], w2e[:, e, :], w_t[:, 2, :], ALU.add).then_inc(S["prep_sum"], 1)

            pool.wait_ge(S["v_ready"], NB)
            v_copy(0, 0)

            def after_max(h, more):
                pool.wait_ge(m_ready, h + 1)
                mparts_copy(h)
                if more:
                    left_max_copy(h + 1)

            def head(h, par, more):
                pool.wait_ge(pv_done, h * PAIRS + PVC)
                v_copy(1 - par, h + 1)
                after_max(h + 1, more)

            after_max(0, True)

            pool.wait_ge(S["prep_ready"], WSTEPS)
            bt = b_t[:, :, :].rearrange("p m f -> p (m f)")
            step(g.tensor_copy(b_split[:, 0, :], bt))
            step(g.tensor_tensor(b_res, bt, b_split[:, 0, :], ALU.subtract))
            step(g.tensor_copy(b_split[:, 1, :], b_res))
            g.tensor_tensor(b_split[:, 2, :], b_res, b_split[:, 1, :], ALU.subtract).then_inc(S["bt_split"], 1)

            with pool.Fori(0, H // 2 - 1) as i:
                head(i * 2, 0, True)
                head(i * 2 + 1, 1, True)
            head(H - 2, 0, False)

            for n_h in range(2 * E * FC):
                u, c = n_h // FC, n_h % FC
                pool.wait_ge(S["silu_ready"], n_h + 1)
                if c == 0 and u >= 2:
                    pool.wait_ge(S["down_ps"], u - 1)
                g.tensor_tensor(act_t[:, u % 2, c, :], uv_t[:, n_h % HR, 0, :], uv_t[:, n_h % HR, 1, :],
                                ALU.mult).then_inc(S["act_ready"], 1)

        @block.scalar
        def _(act):
            s = nc.scalar
            vectors = ((q_b, D), (ln_g, D), (ln_b, D), (tln_g, L), (tln_b, L), (norm_w, D))

            def load_vector(i):
                v, w = vectors[i]
                act.dma_start(cols[0:w, i:i + 1], v.rearrange("(p a) -> p a", a=1)).then_inc(S["cols_in"], 16)

            act.dma_start(qw_sb[:, :], q_w).then_inc(S["qw_in"], 16)
            load_vector(0)
            load_vector(1)
            act.wait_ge(S["bn_done"], 1)
            s.activation(rx[:, 0, :], mvx[:, :, 1], ACT.Sqrt).then_inc(S["sd_done"], 1)
            for i in range(2, 6):
                load_vector(i)
            act.dma_start(ctx_left[:, :], ctx_in[0, NM:NK, :]).then_inc(S["ctxl_in"], 16)
            act.wait_ge(S["bn_done"], 2)
            s.activation(rx[:, 1, :], mvx[:, :, 1], ACT.Sqrt).then_inc(S["sd_done"], 1)
            act.wait_ge(S["cols_in"], 6 * 16)
            for hf in range(2):
                act.wait_ge(S["xt_ready"], hf + 1)
                s.activation(xn_t[:, hf * HALF:(hf + 1) * HALF], SCB[:, hf, :], ACT.Identity,
                             bias=cols[:, LNB:LNB + 1], scale=cols[:, LNG:LNG + 1]).then_inc(S["xn_ready"], 1)
            act.wait_ge(S["cvar_done"], 1)
            s.activation(statl[:, 2:3], statl[:, 1:2], ACT.Sqrt)
            s.activation(stat[:, 2, 0:TE], stat[:, 1, 0:TE], ACT.Sqrt).then_inc(S["csd_done"], 1)

            def kn_evac(gi):
                n0, w = group(gi)
                act.wait_ge(S["ct_ps"], gi + 1)
                if gi >= KNR:
                    act.wait_ge(S["v_ps"], gi - KNR + 1)
                s.activation(kn_t[0:L, gi % KNR, 0:w], SCB[0:L, 0, 0:w], ACT.Identity,
                             bias=cols[0:L, TLB:TLB + 1], scale=cols[0:L, TLG:TLG + 1]).then_inc(S["kn_ready"], 1)

            act.wait_ge(S["q_ready"], 1)
            s.activation(q_split[:, 0, :], q_t, ACT.Copy).then_inc(S["q_hi"], 1)
            kn_evac(0)
            act.wait_ge(S["lt_ps"], 1)
            s.activation(knl_t[0:L, :], AC[0:L, 0:NL], ACT.Identity, bias=cols[0:L, TLB:TLB + 1],
                         scale=cols[0:L, TLG:TLG + 1]).then_inc(S["lt_ready"], 1)
            act.wait_ge(S["q_res"], 1)
            s.activation(q_split[:, 1, :], split_r[:, :, :].rearrange("p i n -> p (i n)"), ACT.Copy).then_inc(S["q_mid"], 1)

            def ctx_norm(gi):
                for j in range(gi * GT, min(gi * GT + GT, NT)):
                    ins = s.activation(ctx_sb[:, j, :], ctx_sb[:, j, :], ACT.Identity,
                                       bias=stat[:, 1, j:j + 1], scale=stat[:, 3, j:j + 1])
                ins.then_inc(S["cn_act_ready"], 1)

            def k_first(gi):
                n0, w = group(gi)
                c, o = gi // 2, (gi % 2) * MB
                act.wait_ge(S["k_ps"], gi + 1)
                if gi >= 4:
                    act.wait_ge(S["k_stored"], 48 * (gi - 3))
                s.activation(k_split[c % 2][:, 0, o:o + w], SCB[:, 2 + gi % 2, 0:w], ACT.Copy).then_inc(S["k_hi"], 1)
                act.wait_ge(S["q_lo"], 1)
                if gi >= 2:
                    act.wait_ge(S["k_lo"], gi - 1)
                s.activation(split_r[:, gi % 2, 0:w], SCB[:, 2 + gi % 2, 0:w], ACT.Copy).then_inc(S["k_copied"], 1)

            def k_second(gi):
                n0, w = group(gi)
                c, o = gi // 2, (gi % 2) * MB
                act.wait_ge(S["k_res"], gi + 1)
                s.activation(k_split[c % 2][:, 1, o:o + w], split_r[:, gi % 2, 0:w], ACT.Copy).then_inc(S["k_mid"], 1)

            def v_evac(gi):
                n0, w = group(gi)
                act.wait_ge(S["v_ps"], gi + 1)
                s.activation(v_all[:, gi * GT:gi * GT + w // 128, :].rearrange("p j d -> p (j d)"),
                             AC[:, 0:w], ACT.Copy).then_inc(S["v_ready"], 1)

            def prep_evac(k):
                act.wait_ge(S["prep_ps"], k + 1)
                bank = SCB[:, 1, :]
                if k < 3:
                    ins = s.activation(w_t[:, k, :], bank, ACT.Copy)
                elif k < 5:
                    ins = s.activation(b_t[:, k - 3, :], bank, ACT.Copy, scale=LORA)
                elif k == 5:
                    s.activation(b2_t[:, :], bank[:, 0:D], ACT.Copy)
                    s.activation(a_t[:, :, :].rearrange("p m n -> p (m n)"), bank[:, 128:128 + 2 * E * R], ACT.Copy)
                    ins = s.activation(gate_t[:, :], bank[:, 384:384 + E], ACT.Copy)
                else:
                    ins = s.activation(w2e[:, k - 6, :], bank, ACT.Copy, scale=LORA)
                ins.then_inc(S["prep_ready"], 1)

            for st in range(1, WSTEPS + LAG + 1):
                if st < NB:
                    kn_evac(st)
                if st <= NB:
                    k_first(st - 1)
                if st == 2:
                    act.wait_ge(S["cvar_done"], 2)
                    s.activation(stat[:, 2, TE:NT], stat[:, 1, TE:NT], ACT.Sqrt).then_inc(S["csd_done"], 1)
                if EARLY <= st + 1 < NB:
                    if st + 1 == EARLY:
                        act.wait_ge(S["cstat_ready"], 2)
                    ctx_norm(st + 1)
                if 0 <= st - LAG - 1 < NB:
                    v_evac(st - LAG - 1)
                if st <= NB:
                    k_second(st - 1)
                if 0 <= st - LAG - 1 < WSTEPS:
                    prep_evac(st - LAG - 1)

            def m_rows(par, h):
                act.wait_ge(mt_done, h + 1)
                s.activation(q_exp[par][0:2, :], MX[0:2, 2, :].bitcast(bf16), ACT.Copy).then_inc(mrow_ready, 1)

            act.sem_inc(exp_done, 2)
            act.sem_inc(acc_free, 1)
            m_rows(0, 0)

            def head(h, par, next_max):
                for j in range(NT):
                    if not next_max and j == LEFT_AT:
                        act.wait_ge(S["lz_ready"], 1)
                        s.activation(left_p, left_scores[:, :, :], ACT.Exp).then_inc(S["lp_ready"], 1)
                    if not next_max and j == LEFT_AT + 4:
                        act.wait_ge(S["lpt_ps"], 1)
                        s.activation(left_pt, MX[0:H * NL, 0:2, :].rearrange("p a b -> p (a b)"),
                                     ACT.Copy).then_inc(S["lpt_ready"], 1)
                    if j == ROWS_AT and next_max:
                        m_rows(1 - par, h + 1)
                    act.wait_ge(st_done, h * NT + j + 1)
                    act.wait_ge(pv_done, h * PAIRS + (j - PR) // 2 + 1 + PVC)
                    s.activation(probs[:, j % PR, :], SC[:, j % 2, :], ACT.Exp).then_inc(exp_done, 1)
                act.wait_ge(pv_done, (h + 1) * PAIRS + PVC)
                act.wait_ge(y_stored[par], 32 * (h - par) + 64)
                s.activation(sums[par][:, :], AC[:, :], ACT.Copy).then_inc(acc_free, 1)

            with act.Fori(0, H // 2 - 1) as i:
                head(i * 2, 0, True)
                head(i * 2 + 1, 1, True)
            head(H - 2, 0, True)
            head(H - 1, 1, False)

            act.wait_ge(S["var1_done"], 1)
            s.activation(rx[:, 0, :], mvx[:, :, 1], ACT.Sqrt).then_inc(S["sd1_done"], 1)
            for a in range(TA):
                act.wait_ge(S["zt_ready"], a + 1)
                ins = s.activation(tmp[:, a, :], zt[:, a, :], ACT.Square, accum_out=gs[:, 0, a:a + 1])
            ins.then_inc(S["sq_done"], 1)
            act.wait_ge(S["ms_done"], 1)
            s.activation(rx[:, 1, :], gs[:, 0, :], ACT.Sqrt).then_inc(S["sd2_done"], 1)
            for hf in range(2):
                act.wait_ge(S["tt_ps"], hf + 1)
                s.activation(t_t[:, hf * HALF:(hf + 1) * HALF], SCB[:, hf, :], ACT.Copy,
                             scale=cols[:, NW:NW + 1]).then_inc(S["tt_ready"], 1)
            for m in range(2):
                act.wait_ge(S["la_ps"], m + 1)
                s.activation(la_split[m][:, 0, :], SC[:, 1 - m, :], ACT.Copy).then_inc(S["la_hi"], 1)
            for m in range(2):
                act.wait_ge(S["la_res_done"], m + 1)
                s.activation(la_split[m][:, 1, :], la_res[m], ACT.Copy).then_inc(S["la_mid"], 1)
            act.wait_ge(S["lg_sub"], 1)
            s.activation(gt[:, 1, :, :], gt[:, 0, :, :], ACT.Exp).then_inc(S["lg_exp"], 1)
            for n_b in range(4 * FC):
                hf, c, m = n_b // (2 * FC), n_b // 2 % FC, n_b % 2
                act.wait_ge(S["base_ps"], n_b + 1)
                s.activation(base[hf][:, c, m, :], SCB[:, n_b % 4, :], ACT.Copy).then_inc(S["base_ready"], 1)
            for n_h in range(2 * E * FC):
                act.wait_ge(S["uv_ready"], n_h + 1)
                s.activation(uv_t[:, n_h % HR, 0, :], uv_t[:, n_h % HR, 0, :], ACT.Silu).then_inc(S["silu_ready"], 1)

        @block.vector
        def _(dve):
            v = nc.vector
            n = 0

            def link(ins):
                nonlocal n
                n += 1
                ins.then_inc(dve_link, 1)
                dve.wait_ge(dve_link, n)

            def stats(src, eps):
                for a in range(TA):
                    v.bn_stats(bnx[:, a, :], src[:, a, :])
                link(v.memset(statl[:, 3:4], 0.0))
                for a in range(TA):
                    v.bn_aggr(mvx[:, a, :], bnx[:, a, :])
                link(v.memset(statl[:, 3:4], 0.0))
                v.tensor_scalar(mvx[:, :, 1], mvx[:, :, 1], eps, None, ALU.add).then_inc(S["bn_done"], 1)

            def normalise(dst, src, i):
                link(v.reciprocal(rx[:, i, :], rx[:, i, :]))
                for a in range(TA):
                    ins = v.tensor_scalar(dst[:, a, :], src[:, a, :], mvx[:, a, 0:1], rx[:, i, a:a + 1],
                                          ALU.subtract, ALU.mult)
                link(ins)

            dve.wait_ge(S["x_in"], 16)
            stats(x_sb, LN_EPS)
            dve.wait_ge(S["sd_done"], 1)
            normalise(z_sb, x_sb, 0)
            stats(z_sb, LN_EPS)
            dve.wait_ge(S["sd_done"], 2)
            link(v.reciprocal(rx[:, 1, :], rx[:, 1, :]))
            for a in range(TA):
                v.tensor_scalar(z_sb[:, a, :], z_sb[:, a, :], mvx[:, a, 0:1], rx[:, 1, a:a + 1],
                                ALU.subtract, ALU.mult).then_inc(S["z_ready"], 1)

            def ctx_stats(j0, j1):
                mean, var, t = stat[:, 0, j0:j1], stat[:, 1, j0:j1], stat[:, 3, j0:j1]
                link(v.tensor_tensor(mean, bn[:, j0:j1, 1], bn[:, j0:j1, 4], ALU.add))
                link(v.tensor_tensor(var, bn[:, j0:j1, 1], bn[:, j0:j1, 4], ALU.subtract))
                link(v.tensor_tensor(var, var, var, ALU.mult))
                link(v.tensor_tensor(t, bn[:, j0:j1, 2], bn[:, j0:j1, 5], ALU.add))
                link(v.tensor_scalar(t, t, 1.0 / L, LN_EPS, ALU.mult, ALU.add))
                link(v.tensor_scalar(mean, mean, 0.5, None, ALU.mult))
                v.scalar_tensor_tensor(var, var, 0.25, t, ALU.mult, ALU.add).then_inc(S["cvar_done"], 1)

            def ctx_norm(gi):
                for j in range(gi * GT, gi * GT + GT):
                    ins = v.tensor_scalar(ctx_sb[:, j, :], ctx_sb[:, j, :], stat[:, 0, j:j + 1],
                                          stat[:, 3, j:j + 1], ALU.subtract, ALU.mult)
                ins.then_inc(S["cn_ready"], 1)

            def bn_tiles(j0, j1):
                for j in range(j0, j1):
                    ins = v.bn_stats(bn[:, j, :], ctx_sb[:, j, :])
                return ins

            dve.wait_ge(S["ctx_in_s"], 16)
            dve.wait_ge(S["ctxl_in"], 16)
            bn_tiles(0, TE)
            link(v.bn_stats(bnl[:, :], ctx_left[:, :]))
            link(v.bn_aggr(statl[:, 0:2], bnl[:, :]))
            link(v.tensor_scalar(statl[:, 1:2], statl[:, 1:2], LN_EPS, None, ALU.add))
            ctx_stats(0, TE)
            dve.wait_ge(S["q_ps"], 1)
            dve.wait_ge(S["cols_in"], 6 * 16)
            link(v.tensor_scalar(q_t, SC[:, 1, :], cols[:, QB:QB + 1], QSCALE, ALU.add, ALU.mult))
            dve.sem_inc(S["q_ready"], 1)
            dve.wait_ge(S["csd_done"], 1)
            link(v.reciprocal(stat[:, 3, 0:TE], stat[:, 2, 0:TE]))
            link(v.reciprocal(statl[:, 3:4], statl[:, 2:3]))
            link(v.tensor_scalar(ctx_left[:, :], ctx_left[:, :], statl[:, 0:1], statl[:, 3:4],
                                 ALU.subtract, ALU.mult))
            dve.sem_inc(S["cstat_ready"], 1)
            ctx_norm(0)
            dve.wait_ge(S["q_hi"], 1)
            v.tensor_tensor(split_r[:, :, :].rearrange("p i n -> p (i n)"), q_t, q_split[:, 0, :],
                            ALU.subtract).then_inc(S["q_res"], 1)
            ctx_norm(1)
            ctx_norm(2)
            ctx_norm(3)
            dve.wait_ge(S["ctx_in_s"], 2 * 16)
            TM = (TE + NT) // 2
            link(bn_tiles(TE, TM))

            def left_keys(st):
                if st == 1:
                    dve.wait_ge(S["lk_ps"], 1)
                    dve.wait_ge(S["masks0_ready"], 1)
                    link(v.tensor_copy(kl_t[:, :], AC[:, 8:8 + NL]))
                    v.tensor_tensor(kl_bd[:, :, :], kl_t[:, :].unsqueeze(1).to_broadcast([128, H, NL]),
                                    head_mask[:, :].unsqueeze(2).to_broadcast([128, H, NL]),
                                    ALU.mult).then_inc(S["lk_ready"], 1)
                elif st == 2:
                    dve.wait_ge(S["lv_ps"], 1)
                    v.tensor_tensor(v_left[:, 0:D].rearrange("p (h d) -> p h d", h=H),
                                    AC[0:H * NL, 128:256].rearrange("p (h d) -> p h d", h=H),
                                    left_mask[:, :].unsqueeze(2).to_broadcast([H * NL, H, DH]), ALU.mult)
                    v.tensor_copy(v_left[:, D:D + H], left_mask[:, :]).then_inc(S["lv_ready"], 1)
                elif st == 3:
                    dve.wait_ge(S["ls_ps"], 1)
                    link(v.tensor_copy(left_scores[:, :, :].rearrange("p a n -> p (a n)"), AC[:, :]))
                    v.tensor_reduce(left_max[:, :, :], left_scores[:, :, :].rearrange("p a (h n) -> p a h n", n=NL),
                                    axis=AX.X, op=ALU.max).then_inc(S["ls_ready"], 1)

            def max_block(h, b):
                kb, a = b // TA, b % TA
                w = min(MB, NM - kb * MB)
                dve.wait_ge(mb_done, h * MAXB + b + 1)
                v.tensor_reduce(blockmax[:, a, kb:kb + 1], MX[:, mx_bank(b), 0:w], axis=AX.X,
                                op=ALU.max).then_inc(mx_done, 1)

            def max_final(h):
                dve.wait_ge(mx_done, (h + 1) * MAXB)
                dve.wait_ge(lm_ready, h + 1)
                dve.wait_ge(ms_ready, h + 1)
                v.tensor_reduce(negmax[:, :], blockmax[:, :, :], axis=AX.X, op=ALU.max,
                                negate=True).then_inc(max_link, 1)
                dve.wait_ge(max_link, h * 2 + 1)
                v.tensor_copy(mparts[:, :, 0], negmax[:, :]).then_inc(max_link, 1)
                dve.wait_ge(max_link, h * 2 + 2)
                v.tensor_tensor(mparts[:, :, 1], negmax[:, :], mparts[:, :, 0], ALU.subtract).then_inc(m_ready, 1)

            dve.sem_inc(ms_ready, 1)
            for st in range(NB + LAG):
                left_keys(st)
                if st == 1:
                    link(bn_tiles(TM, NT))
                    ctx_stats(TE, NT)
                if st == 2:
                    dve.wait_ge(S["csd_done"], 2)
                    link(v.reciprocal(stat[:, 3, TE:NT], stat[:, 2, TE:NT]))
                    v.scalar_tensor_tensor(stat[:, 1, TE:NT], stat[:, 0, TE:NT], -1.0, stat[:, 3, TE:NT],
                                           ALU.mult, ALU.mult).then_inc(S["cstat_ready"], 1)
                if st >= MLAG and st - MLAG < NB:
                    for b in range((st - MLAG) * TA, (st - MLAG + 1) * TA):
                        max_block(0, b)
            max_final(0)
            for b in range(AHEAD):
                max_block(1, b)

            def head(h, more):
                for b in range(AHEAD, MAXB):
                    max_block(h + 1, b)
                max_final(h + 1)
                if more:
                    for b in range(AHEAD):
                        max_block(h + 2, b)

            with dve.Fori(0, H // 2 - 1) as i:
                head(i * 2, True)
                head(i * 2 + 1, True)
            head(H - 2, False)

            dve.wait_ge(ms_ready, H + 1)
            lz = left_scores[:, :, :].rearrange("p a (h n) -> p a h n", n=NL)
            for part in range(2):
                m = mparts_all[:, :, :, part].rearrange("p h a -> p a h").unsqueeze(3)
                ins = v.tensor_tensor(lz, lz, m.to_broadcast([128, TA, H, NL]), ALU.add)
                if part == 0:
                    link(ins)
            ins.then_inc(S["lz_ready"], 1)

            dve.wait_ge(y_loaded, 48)
            v.tensor_tensor(y_num[0:D - DH, 0, :], y_num[0:D - DH, 0, :], y_num[0:D - DH, 1, :], ALU.add)
            v.tensor_tensor(y_den[:, 0, :], y_den[:, 0, :], y_den[:, 1, :], ALU.add).then_inc(S["y_sum"], 1)

            for b in range(3):
                dve.wait_ge(S["y_ps"], b + 1)
                a0, a1_ = 3 * b, min(3 * b + 3, TA)
                y = MX[:, b, 0:(a1_ - a0) * H * YW].rearrange("p (a c) -> p a c", c=H * YW)
                t4 = tmp[:, a0:a1_, :].rearrange("p a (h d) -> p a h d", d=DH)
                link(v.reciprocal(rden[:, a0:a1_, :], y[:, :, D:D + H]))
                link(v.tensor_tensor(t4, y[:, :, 0:D].rearrange("p a (h d) -> p a h d", d=DH),
                                     rden[:, a0:a1_, :].unsqueeze(3).to_broadcast([128, a1_ - a0, H, DH]), ALU.mult))
                link(v.tensor_tensor(x_sb[:, a0:a1_, :], x_sb[:, a0:a1_, :], tmp[:, a0:a1_, :], ALU.add))

            for a in range(TA):
                v.bn_stats(bnx[:, a, :], x_sb[:, a, :])
            link(v.memset(statl[:, 3:4], 0.0))
            for a in range(TA):
                v.bn_aggr(mvx[:, a, :], bnx[:, a, :])
            link(v.memset(statl[:, 3:4], 0.0))
            v.tensor_scalar(mvx[:, :, 1], mvx[:, :, 1], LN_EPS, None, ALU.add).then_inc(S["var1_done"], 1)
            dve.wait_ge(S["sd1_done"], 1)
            link(v.reciprocal(rx[:, 0, :], rx[:, 0, :]))
            for a in range(TA):
                v.tensor_scalar(zt[:, a, :], x_sb[:, a, :], mvx[:, a, 0:1], rx[:, 0, a:a + 1],
                                ALU.subtract, ALU.mult).then_inc(S["zt_ready"], 1)
            dve.wait_ge(S["sq_done"], 1)
            v.tensor_scalar(gs[:, 0, :], gs[:, 0, :], 1.0 / D, RMS_EPS, ALU.mult, ALU.add).then_inc(S["ms_done"], 1)
            dve.wait_ge(S["sd2_done"], 1)
            link(v.reciprocal(rx[:, 1, :], rx[:, 1, :]))
            for hf in range(2):
                z = zt[:, hf * TA // 2:(hf + 1) * TA // 2, :]
                v.tensor_tensor(z, z, rx[:, 1, hf * TA // 2:(hf + 1) * TA // 2].unsqueeze(2).to_broadcast(
                    [128, TA // 2, D]), ALU.mult).then_inc(S["tn_ready"], 1)

            for m in range(2):
                dve.wait_ge(S["la_hi"], m + 1)
                v.tensor_tensor(la_res[m], SC[:, 1 - m, :], la_split[m][:, 0, :], ALU.subtract).then_inc(S["la_res_done"], 1)
            for m in range(2):
                dve.wait_ge(S["la_mid"], m + 1)
                v.tensor_tensor(la_split[m][:, 2, :], la_res[m], la_split[m][:, 1, :], ALU.subtract).then_inc(S["la_ready"], 1)

            def over_e(col):
                return col.unsqueeze(2).to_broadcast([128, TA, E])

            def e_max(dst, src):
                link(v.tensor_reduce(dst, src, axis=AX.X, op=ALU.max))

            lg = MX[:, 2, 0:TA * E].rearrange("p (a e) -> p a e", e=E)
            first_b = first[:, :].unsqueeze(1).to_broadcast([128, TA, E])
            dve.wait_ge(S["masks_ready"], 1)
            dve.wait_ge(S["lg_ps"], 1)
            e_max(gs[:, 1, :], lg)
            v.tensor_tensor(gt[:, 0, :, :], lg, over_e(gs[:, 1, :]), ALU.subtract).then_inc(S["lg_sub"], 1)
            dve.wait_ge(S["lg_exp"], 1)
            link(v.tensor_reduce(gs[:, 2, :], gt[:, 1, :, :], axis=AX.X, op=ALU.add))
            link(v.reciprocal(gs[:, 2, :], gs[:, 2, :]))
            link(v.tensor_tensor(gt[:, 1, :, :], gt[:, 1, :, :], over_e(gs[:, 2, :]), ALU.mult))
            for top in range(2):
                pr, best = gt[:, 1 + top, :, :], gs[:, 3 + top, :]
                choice = gt[:, 3 + top, :, :]
                e_max(best, pr)
                link(v.tensor_tensor(choice, pr, over_e(best), ALU.is_equal))
                link(v.tensor_tensor(choice, choice, first_b, ALU.mult))
                e_max(gs[:, 5, :], choice)
                link(v.tensor_tensor(choice, choice, over_e(gs[:, 5, :]), ALU.is_equal))
                if top == 0:
                    link(v.scalar_tensor_tensor(gt[:, 2, :, :], choice, -2.0, pr, ALU.mult, ALU.add))
            link(v.tensor_tensor(gs[:, 6, :], gs[:, 3, :], gs[:, 4, :], ALU.add))
            link(v.reciprocal(gs[:, 6, :], gs[:, 6, :]))
            for top in range(2):
                link(v.tensor_tensor(gs[:, 3 + top, :], gs[:, 3 + top, :], gs[:, 6, :], ALU.mult))
                link(v.tensor_tensor(gt[:, 3 + top, :, :], gt[:, 3 + top, :, :], over_e(gs[:, 3 + top, :]), ALU.mult))
            link(v.tensor_tensor(gt[:, 5, :, :], gt[:, 3, :, :], gt[:, 4, :, :], ALU.add))

            def combine(u):
                e, hf = u // 2, u % 2
                dve.wait_ge(S["down_ps"], u + 1)
                for q in range(4):
                    a = hf * 4 + q
                    ins = v.scalar_tensor_tensor(x_sb[:, a, :], MX[:, u % 2, q * 128:(q + 1) * 128],
                                                 gt[:, 5, a, e:e + 1], x_sb[:, a, :], ALU.mult, ALU.add)
                link(ins)
                dve.sem_inc(S["down_used"], 1)

            for u in range(2 * E):
                for c in range(FC):
                    n_h = u * FC + c
                    dve.wait_ge(S["h_ps"], n_h + 1)
                    if n_h >= HR:
                        dve.wait_ge(S["act_ready"], n_h - HR + 1)
                    if n_h == 0:
                        dve.wait_ge(S["base_ready"], 4 * FC)
                    v.tensor_tensor(uv_t[:, n_h % HR, :, :].rearrange("p m t -> p (m t)"), SC[:, n_h % 2, :],
                                    base[u % 2][:, c, :, :].rearrange("p m t -> p (m t)"),
                                    ALU.add).then_inc(S["uv_ready"], 1)
                    if c == 2 and u >= 2:
                        combine(u - 2)
            combine(2 * E - 2)
            combine(2 * E - 1)
            dve.sem_inc(S["out_ready"], 1)

        @block.tensor
        def _(pe):
            p = nc.tensor
            pe.wait_ge(S["const_ready"], 1)
            for a in range(TA):
                pe.wait_ge(S["z_ready"], a + 1)
                ins = p.transpose(SC[:, 0, a * 128:(a + 1) * 128], z_sb[:, a, :], ident[:, :])
                if a % 4 == 3:
                    ins.then_inc(S["xt_ready"], 1)
            pe.wait_ge(S["qw_in"], 16)
            for hf in range(2):
                pe.wait_ge(S["xn_ready"], hf + 1)
                ins = p.matmul(SC[:, 1, hf * HALF:(hf + 1) * HALF], qw_sb[:, :],
                               xn_t[:, hf * HALF:(hf + 1) * HALF], start=True, stop=True)
            ins.then_inc(S["q_ps"], 1)

            def ctx_transpose(gi):
                if gi < EARLY:
                    pe.wait_ge(S["cn_ready"], gi + 1)
                else:
                    pe.wait_ge(S["cn_act_ready"], gi - EARLY + 1)
                if gi >= 1:
                    pe.wait_ge(S["kn_ready"], gi)
                for j in range(gi * GT, min(gi * GT + GT, NT)):
                    o = (j - gi * GT) * 128
                    ins = p.transpose(SCB[0:L, 0, o:o + 128], ctx_sb[:, j, :], ident[:, :])
                ins.then_inc(S["ct_ps"], 1)

            def k_project(gi):
                n0, w = group(gi)
                pe.wait_ge(S["kn_ready"], gi + 1)
                if gi >= 2:
                    pe.wait_ge(S["k_copied"], gi - 1)
                p.matmul(SCB[:, 2 + gi % 2, 0:w], kw_sb[:, :], kn_t[:, gi % KNR, 0:w],
                         start=True, stop=True).then_inc(S["k_ps"], 1)

            def v_project(gi):
                n0, w = group(gi)
                if gi == 0:
                    pe.wait_ge(S["ls_ready"], 1)
                else:
                    pe.wait_ge(S["v_ready"], gi)
                for o in range(0, w, 128):
                    ins = p.matmul(AC[:, o:o + 128], kn_t[:, gi % KNR, o:o + 128], vw_sb[:, :],
                                   start=True, stop=True)
                ins.then_inc(S["v_ps"], 1)

            def prep(k):
                bank = SCB[:, 1, :]
                if k == 0:
                    pe.wait_ge(S["ffn_in"], 16 * 16)
                else:
                    pe.wait_ge(S["prep_ready"], k)
                if k < 3:
                    for c in range(FC):
                        ins = p.transpose(bank[:, c * 128:(c + 1) * 128], w_nat[:, k, c * 128:(c + 1) * 128], ident[:, :])
                elif k < 5:
                    for c in range(FC):
                        ins = p.transpose(bank[:, c * 128:(c + 1) * 128], b_nat[:, k - 3, c, :], ident[:, :])
                elif k == 5:
                    p.transpose(bank[:, 0:D], b2_nat[:, :, :].rearrange("p e r -> p (e r)"), ident[:, :])
                    for m in range(2):
                        p.transpose(bank[:, 128 * (m + 1):128 * (m + 2)], a_nat[:, m, :], ident[:, :])
                    ins = p.transpose(bank[:, 384:384 + E], gate_nat[:, :], ident[0:E, 0:E])
                else:
                    e = k - 6
                    pe.wait_ge(S["masked_ready"], e + 1)
                    for c in range(FC):
                        ins = p.matmul(bank[:, c * 128:(c + 1) * 128], a2_nat[:, c * 128:(c + 1) * 128],
                                       masked[:, e % 2, :], start=True, stop=True)
                ins.then_inc(S["prep_ps"], 1)

            def max_block(par, h, b):
                kb, a = b // TA, b % TA
                n0, w = group(kb)
                if a == 0 and isinstance(h, int) and h == 0:
                    pe.wait_ge(kg_loaded[kb % 2], 48 * (kb // 2 + 1))
                elif a == 0 and kb % 2 == 0:
                    pe.wait_ge(k_loaded[par][kb // 2], (h + par) * 24)
                if b == 0 and not (isinstance(h, int) and h == 1):
                    pe.wait_ge(qm_loaded, (h + 1) * 16)
                at_start = isinstance(h, int) and h == 0
                if b == 4:
                    if not at_start:
                        pe.wait_ge(mrow_ready, h)
                elif b in (2, 3):
                    pe.wait_ge(mx_done, h * MAXB + b - 1)
                elif not (at_start and b < 2):
                    pe.wait_ge(mx_done, h * MAXB + b - 2)
                p.matmul(MX[:, mx_bank(b), 0:w], q_max[par][0:KR, a * 128:(a + 1) * 128],
                         k_op[par][0:KR, n0:n0 + w], start=True, stop=True).then_inc(mb_done, 1)

            def max_transpose(h):
                pe.wait_ge(m_ready, h + 1)
                for a in range(TA):
                    ins = p.transpose(MX[0:2, 2, :].bitcast(bf16)[:, a * 128:(a + 1) * 128], mparts[:, a, :],
                                      ident_b[:, :])
                ins.then_inc(mt_done, 1)

            ctx_transpose(0)
            pe.wait_ge(S["csd_done"], 1)
            pe.wait_ge(S["cstat_ready"], 1)
            p.transpose(AC[0:L, 0:NL], ctx_left[:, :], ident[0:NL, 0:NL]).then_inc(S["lt_ps"], 1)
            pe.wait_ge(S["q_ready"], 1)
            pe.wait_ge(S["w_in"], 4 * 16)
            for st in range(NB + LAG):
                stream = []
                if st >= MLAG and st - MLAG < NB:
                    stream = [lambda b=b: max_block(0, 0, b) for b in range((st - MLAG) * TA, (st - MLAG + 1) * TA)]
                if st == MLAG:
                    pe.wait_ge(S["rows_ready"], 1)
                if st + 1 < NB and not stream:
                    ctx_transpose(st + 1)
                for block in stream[0:2]:
                    block()
                if st < NB:
                    k_project(st)
                for block in stream[2:4]:
                    block()
                if st + 1 < NB and stream:
                    ctx_transpose(st + 1)
                if st >= LAG:
                    v_project(st - LAG)
                for block in stream[4:6]:
                    block()
                if st >= LAG:
                    prep(st - LAG)
                for block in stream[6:8]:
                    block()
                if st == 0:
                    pe.wait_ge(S["lt_ready"], 1)
                    p.matmul(AC[:, 8:8 + NL], kw_sb[:, :], knl_t[:, :], start=True, stop=True).then_inc(S["lk_ps"], 1)
                elif st == 1:
                    pe.wait_ge(S["lk_ready"], 1)
                    pe.wait_ge(S["lrep_ready"], 1)
                    p.matmul(AC[0:H * NL, 128:256], knl_rep[:, :, :].rearrange("p h n -> p (h n)"), vw_sb[:, :],
                             start=True, stop=True).then_inc(S["lv_ps"], 1)
                elif st == 2:
                    pe.wait_ge(S["lv_ready"], 1)
                    for a in range(TA):
                        ins = p.matmul(AC[:, a * H * NL:(a + 1) * H * NL], q_t[:, a * 128:(a + 1) * 128],
                                       kl_bd[:, :, :].rearrange("p h n -> p (h n)"), start=True, stop=True)
                    ins.then_inc(S["ls_ps"], 1)
            for k in range(NB, WSTEPS):
                prep(k)
            pe.wait_ge(S["rows_ready"], 2)
            max_transpose(0)
            pe.wait_ge(S["prep_ready"], WSTEPS)
            pe.wait_ge(S["k_copied"], NB)
            pe.wait_ge(S["v_ready"], NB)
            pe.sem_inc(pv_done, PVC)

            def scores(par, h, j):
                if j == 0:
                    pe.wait_ge(mrow_ready, h + 1)
                    pe.wait_ge(q_loaded, (h + 1) * 16)
                pe.wait_ge(exp_done, h * NT + j + 1)
                for hf in range(2):
                    ins = p.matmul(SC[:, j % 2, hf * HALF:(hf + 1) * HALF], k_op[par][0:KR, j * 128:(j + 1) * 128],
                                   q_exp[par][0:KR, hf * HALF:(hf + 1) * HALF], start=True, stop=True)
                ins.then_inc(st_done, 1)

            def v_products(par, h, k):
                if k == 0:
                    pe.wait_ge(vh_ready, h + 1)
                    pe.wait_ge(acc_free, h + 1)
                pe.wait_ge(exp_done, h * NT + 2 * k + 2 + 2)
                for q in range(4):
                    j, hf = 2 * k + q // 2, q % 2
                    ins = p.matmul(AC[32 * q:32 * q + VW, :], v_head[par][:, j, :],
                                   probs[:, j % PR, hf * HALF:(hf + 1) * HALF],
                                   start=(k == 0), stop=(k == PAIRS - 1))
                ins.then_inc(pv_done, 1)

            def left_transposes():
                pe.wait_ge(S["lp_ready"], 1)
                for a in range(TA):
                    ins = p.transpose(MX[0:H * NL, a // 4, (a % 4) * 128:(a % 4 + 1) * 128], left_p[:, a, :],
                                      ident[:, :])
                ins.then_inc(S["lpt_ps"], 1)

            def y_products(a):
                if a == 0:
                    pe.wait_ge(S["lpt_ready"], 1)
                    pe.wait_ge(mrow_ready, H)
                    pe.wait_ge(S["y_sum"], 1)
                q = slice(a * 128, (a + 1) * 128)
                if a % 3 == 0:
                    w = min(3, TA - a) * H * YW
                    p.matmul(MX[:, a // 3, 0:w], q_max[1][0:QROW, 0:128], k_op[1][0:QROW, 0:w],
                             start=True, stop=False, skip_group_check=True)
                p.matmul(y_tile(a, 0, H * YW), left_pt[:, q], v_left[:, :],
                         start=False, stop=False, skip_group_check=True)
                p.matmul(y_tile(a, 0, D), y_num[0:D - DH, 0, q], ident[0:D - DH, :],
                         start=False, stop=False, skip_group_check=True)
                p.matmul(y_tile(a, D, D + H), y_den[:, 0, q], ident[0:H - 1, 0:H],
                         start=False, stop=False, skip_group_check=True)

            def y_last(a):
                q, hf = slice(a % 4 * 128, (a % 4 + 1) * 128), a // 4
                p.matmul(y_tile(a, D - DH, D), sums[1][:, q], sum_sel[:, hf, 0:DH],
                         start=False, stop=False, skip_group_check=True)
                return p.matmul(y_tile(a, D + H - 1, D + H), sums[1][:, q], sum_sel[:, hf, DH:YW],
                                start=False, stop=True, skip_group_check=True)

            def head(par, h, next_max, more, begun=AHEAD):
                stream = []
                if not next_max:
                    stream = [lambda: None] * 12 + [left_transposes] + [lambda: None] * 46
                    for a in range(TA):
                        stream += [lambda a=a: y_products(a), lambda: None]
                else:
                    stream += [lambda b=b: max_block(1 - par, h + 1, b) for b in range(begun, MAXB)]
                    if more:
                        stream += [lambda b=b: max_block(par, h + 2, b) for b in range(2)]
                        stream += [lambda: max_transpose(h + 1)]
                        stream += [lambda b=b: max_block(par, h + 2, b) for b in range(2, AHEAD)]
                    else:
                        stream += [lambda: max_transpose(h + 1)]
                at = 0
                def some(slot):
                    nonlocal at
                    upto = min(-(-(MAXB + 1 + AHEAD - begun) * (slot + 1) // (4 * PAIRS)), len(stream))
                    while at < upto:
                        stream[at]()
                        at += 1
                for k in range(PAIRS):
                    scores(par, h, 2 * k)
                    some(4 * k)
                    scores(par, h, 2 * k + 1)
                    some(4 * k + 1)
                    if k >= 1:
                        v_products(par, h, k - 1)
                    some(4 * k + 3)
                v_products(par, h, PAIRS - 1)

            pe.wait_ge(qm_loaded, 2 * 16)
            head(0, 0, True, True, begun=0)
            head(1, 1, True, True)
            with pe.Fori(1, H // 2 - 1) as i:
                head(0, i * 2, True, True)
                head(1, i * 2 + 1, True, True)
            head(0, H - 2, True, False)
            head(1, H - 1, False, False)

            pe.wait_ge(acc_free, H + 1)
            for a in range(TA):
                ins = y_last(a)
                if a % 3 == 2 or a == TA - 1:
                    ins.then_inc(S["y_ps"], 1)

            for a in range(TA):
                if a % 4 == 0:
                    pe.wait_ge(S["tn_ready"], a // 4 + 1)
                ins = p.transpose(SC[:, 0, a * 128:(a + 1) * 128], zt[:, a, :], ident[:, :])
                if a % 4 == 3:
                    ins.then_inc(S["tt_ps"], 1)
            for m in range(2):
                for hf in range(2):
                    if m == 0:
                        pe.wait_ge(S["tt_ready"], hf + 1)
                    ins = p.matmul(SC[:, 1 - m, hf * HALF:(hf + 1) * HALF], a_t[:, m, :],
                                   t_t[:, hf * HALF:(hf + 1) * HALF], start=True, stop=True)
                ins.then_inc(S["la_ps"], 1)
            for a in range(TA):
                ins = p.matmul(MX[:, 2, a * E:(a + 1) * E], t_t[:, a * 128:(a + 1) * 128], gate_t[:, :],
                               start=True, stop=True)
            ins.then_inc(S["lg_ps"], 1)

            pe.wait_ge(S["la_res_done"], 2)
            for n_b in range(4 * FC):
                hf, c, m = n_b // (2 * FC), n_b // 2 % FC, n_b % 2
                if n_b >= 4:
                    pe.wait_ge(S["base_ready"], n_b - 3)
                p.matmul(SCB[:, n_b % 4, :], w_t[:, m, c * 128:(c + 1) * 128],
                         t_t[:, hf * HALF:(hf + 1) * HALF], start=True, stop=True).then_inc(S["base_ps"], 1)
            pe.wait_ge(S["base_ready"], 4 * FC)
            pe.wait_ge(S["b_loaded"], 16 * 2 * len(TERMS))

            def up(u, c):
                e, hf = u // 2, u % 2
                n_h = u * FC + c
                if n_h >= 2:
                    pe.wait_ge(S["uv_ready"], n_h - 1)
                if hf == 0 and c == 0:
                    pe.wait_ge(la_loaded[e], 6 * 16)
                for m in range(2):
                    ins = p.matmul(SC[:, n_h % 2, m * HALF:(m + 1) * HALF], lb[:, m, e, c * 128:(c + 1) * 128],
                                   la[e][:, m, hf * HALF:(hf + 1) * HALF], start=True, stop=True)
                ins.then_inc(S["h_ps"], 1)

            def down(u, q):
                e = u // 2
                if q == 0:
                    pe.wait_ge(S["act_ready"], (u + 1) * FC)
                    if u >= 2:
                        pe.wait_ge(S["down_used"], u - 1)
                for c in range(FC):
                    ins = p.matmul(MX[:, u % 2, q * 128:(q + 1) * 128], act_t[:, u % 2, c, q * 128:(q + 1) * 128],
                                   w2e[:, e, c * 128:(c + 1) * 128], start=(c == 0), stop=(c == FC - 1))
                if q == 3:
                    ins.then_inc(S["down_ps"], 1)

            pe.wait_ge(S["prep_sum"], E)
            for i in range(2 * E * FC + DOWN_LAG):
                if i < 2 * E * FC:
                    up(i // FC, i % FC)
                if i >= DOWN_LAG:
                    down((i - DOWN_LAG) // 4, (i - DOWN_LAG) % 4)


_INS = ['x', 'ctx_768', 'L0_xattn_q_w', 'L0_xattn_q_b', 'L0_xattn_k_w', 'L0_xattn_k_b', 'L0_xattn_v_w',
        'L0_xattn_v_b', 'L0_xattn_ln_g', 'L0_xattn_ln_b', 'L0_xattn_tln_g', 'L0_xattn_tln_b', 'L0_ffn_norm_w',
        'L0_ffn_w1', 'L0_ffn_w3', 'L0_ffn_w2', 'L0_ffn_gate_w', 'L0_ffn_a1', 'L0_ffn_b1', 'L0_ffn_a3',
        'L0_ffn_b3', 'L0_ffn_a2', 'L0_ffn_b2']


def kernel(**inputs):
    import concourse.bacc as _bacc
    from concourse.bass_utils import run_bass_kernel_spmd as _run

    nc = _bacc.Bacc("TRN2", target_bir_lowering=False, num_devices=1)
    arrays, args = {}, []
    for name in _INS:
        a = np.ascontiguousarray(inputs[name])
        arrays[f"in_{name}"] = a
        args.append(nc.dram_tensor(f"in_{name}", a.shape, mybir.dt.from_np(a.dtype), kind="ExternalInput").ap())
    out = nc.dram_tensor("out_0", tuple(inputs["x"].shape), mybir.dt.float32, kind="ExternalOutput").ap()
    xattn_ffn(nc, *args, out)
    r = _run(nc, [arrays], core_ids=[0])
    return r.results[0]["out_0"]
```
